# Optimizing a Trainium2 kernel written in Bass

```python
import numpy as np
import jax
import jax.numpy as jnp

def _softmax(x, axis=-1):
    return jax.nn.softmax(x, axis=axis)

def _gelu(x):
    return jax.nn.gelu(x, approximate=True)

def _silu(x):
    return jax.nn.silu(x)

def _sigmoid(x):
    return jax.nn.sigmoid(x)

def _layernorm(x, axis=-1, eps=1e-05):
    m = jnp.mean(x, axis=axis, keepdims=True)
    v = jnp.var(x, axis=axis, keepdims=True)
    return (x - m) / jnp.sqrt(v + eps)

def _scatter_add(tgt, idx, src, axis=0):
    return tgt.at[idx].add(src)

def _segment_sum(src, seg, n):
    return jax.ops.segment_sum(src, seg, n)
kernel_name = 'mk_adj_resnorm_d1_adj_r2_11e577'

def setup_inputs(seed: int=0):
    np.random.seed(seed)
    _w = jnp.asarray

    def _rec_inputs():
        import jax
        import jax.numpy as jnp
        _gk = jax.random.key(seed)
        x = -1.394e-06 + 0.9999 * jax.random.normal(jax.random.fold_in(_gk, 1), (8, 1024, 256), jnp.float32)
        _w = (1.0 + jnp.arange(1024, dtype=jnp.float32)) ** (-0.5)
        _w = _w / _w.mean()
        _pij = jnp.clip(0.00390625 * _w[:, None] * _w[None, :], 0.0, 1.0)
        _a = jax.random.uniform(jax.random.fold_in(_gk, 2), (8, 1024, 1024)) < _pij
        adj = _a.astype(jnp.int32)
        return (x, adj)
    x, adj = _rec_inputs()

    def _L0_gnn_setup():
        import jax, jax.numpy as jnp
        import numpy as np
        NEG_INF = -1000000000.0
        NEG_SLOPE = 0.2

        def gat_layer(x, mask, W, a_src, a_dst, bias, concat):
            B, N, _ = x.shape
            H, F = a_src.shape
            xl = (x @ W).reshape(B, N, H, F)
            asrc = jnp.einsum('bnhf,hf->bnh', xl, a_src)
            adst = jnp.einsum('bnhf,hf->bnh', xl, a_dst)
            e = jax.nn.leaky_relu(asrc[:, :, None, :] + adst[:, None, :, :], NEG_SLOPE)
            e = jnp.where(mask[..., None], e, NEG_INF)
            attn = jax.nn.softmax(e, axis=1)
            out = jnp.einsum('bsdh,bshf->bdhf', attn, xl)
            if concat:
                out = out.reshape(B, N, H * F)
            else:
                out = out.mean(axis=2)
            return out + bias
        key = jax.random.key(seed)
        ks = jax.random.split(key, 10)
        B, N, Din, Fh, H, Dout = (8, 512, 256, 128, 4, 256)
        s = 0.05
        return {'adj': jax.random.randint(ks[0], (B, N, N), 0, 2, dtype=jnp.int32), 'x': jax.random.normal(ks[1], (B, N, Din), dtype=jnp.float32), 'W1': jax.random.normal(ks[2], (Din, H * Fh), dtype=jnp.float32) * s, 'att_src1': jax.random.normal(ks[3], (H, Fh), dtype=jnp.float32) * s, 'att_dst1': jax.random.normal(ks[4], (H, Fh), dtype=jnp.float32) * s, 'b1': jax.random.normal(ks[5], (H * Fh,), dtype=jnp.float32) * s, 'W2': jax.random.normal(ks[6], (H * Fh, Dout), dtype=jnp.float32) * s, 'att_src2': jax.random.normal(ks[7], (1, Dout), dtype=jnp.float32) * s, 'att_dst2': jax.random.normal(ks[8], (1, Dout), dtype=jnp.float32) * s, 'b2': jax.random.normal(ks[9], (Dout,), dtype=jnp.float32) * s}
    _L0_gnn_all = _L0_gnn_setup()
    _L0_gnn_in = {k: v for k, v in _L0_gnn_all.items() if k in ('W1', 'att_src1', 'att_dst1', 'b1', 'W2', 'att_src2', 'att_dst2', 'b2')}
    del _L0_gnn_all
    return {'x': x, 'adj': adj, 'L0_gnn_W1': _L0_gnn_in['W1'], 'L0_gnn_att_src1': _L0_gnn_in['att_src1'], 'L0_gnn_att_dst1': _L0_gnn_in['att_dst1'], 'L0_gnn_b1': _L0_gnn_in['b1'], 'L0_gnn_W2': _L0_gnn_in['W2'], 'L0_gnn_att_src2': _L0_gnn_in['att_src2'], 'L0_gnn_att_dst2': _L0_gnn_in['att_dst2'], 'L0_gnn_b2': _L0_gnn_in['b2']}

def reference(x, adj, L0_gnn_W1, L0_gnn_att_src1, L0_gnn_att_dst1, L0_gnn_b1, L0_gnn_W2, L0_gnn_att_src2, L0_gnn_att_dst2, L0_gnn_b2):
    import jax
    import jax.numpy as jnp

    def _L0_gnn_ref(adj, x, W1, att_src1, att_dst1, b1, W2, att_src2, att_dst2, b2):
        import jax, jax.numpy as jnp
        import numpy as np
        NEG_INF = -1000000000.0
        NEG_SLOPE = 0.2

        def gat_layer(x, mask, W, a_src, a_dst, bias, concat):
            B, N, _ = x.shape
            H, F = a_src.shape
            xl = (x @ W).reshape(B, N, H, F)
            asrc = jnp.einsum('bnhf,hf->bnh', xl, a_src)
            adst = jnp.einsum('bnhf,hf->bnh', xl, a_dst)
            e = jax.nn.leaky_relu(asrc[:, :, None, :] + adst[:, None, :, :], NEG_SLOPE)
            e = jnp.where(mask[..., None], e, NEG_INF)
            attn = jax.nn.softmax(e, axis=1)
            out = jnp.einsum('bsdh,bshf->bdhf', attn, xl)
            if concat:
                out = out.reshape(B, N, H * F)
            else:
                out = out.mean(axis=2)
            return out + bias
        B, N, _ = adj.shape
        mask = (adj > 0) | jnp.eye(N, dtype=bool)[None]
        h = jax.nn.elu(gat_layer(x, mask, W1, att_src1, att_dst1, b1, concat=True))
        h = gat_layer(h, mask, W2, att_src2, att_dst2, b2, concat=False)
        return h
    x = _layernorm(x + _L0_gnn_ref(adj, x, L0_gnn_W1, L0_gnn_att_src1, L0_gnn_att_dst1, L0_gnn_b1, L0_gnn_W2, L0_gnn_att_src2, L0_gnn_att_dst2, L0_gnn_b2), axis=-1)
    return x

_drawn_inputs = setup_inputs


def setup_inputs(seed=0):
    import zlib

    import numpy as np

    out = dict(_drawn_inputs(seed))
    spreads = {}
    factors = {'L0_gnn_att_dst1': 3.422, 'L0_gnn_att_dst2': 5.377}
    for name, (base, spread) in spreads.items():
        noise = np.random.default_rng([zlib.crc32(name.encode()), seed]).standard_normal(out[name].shape)
        drawn = base * np.exp(spread * noise) if base else spread * noise
        out[name] = jnp.asarray(drawn.astype(out[name].dtype))
    for name, factor in factors.items():
        out[name] = (out[name] * factor).astype(out[name].dtype)
    return out
```

```python
from contextlib import ExitStack

import concourse.bass as bass
from concourse import mybir

ALU = mybir.AluOpType
ACT = mybir.ActivationFunctionType
AX = mybir.AxisListType
F32 = mybir.dt.float32
I32 = mybir.dt.int32
U8 = mybir.dt.uint8
RMAX = bass.bass_isa.ReduceOp.max

P = 128
SLOPE = 0.2
GAP = 1.0 - SLOPE
RANGE = 86.0
EPS = 1e-5
XR = 4
UNITS = 5


def build_gat(nc, x, adj, W1, att_src1, att_dst1, b1, W2, att_src2, att_dst2, b2, out):
    B, N, D = x.shape
    H, F = att_src1.shape
    HF = H * F
    T = N // P
    KC = D // P
    FC = HF // P
    VW = F + 1
    V2W = D + 2
    S1 = H * T
    SLOTS = UNITS * T
    NA = 2 * H
    assert F == P and T == 8 and KC == 2

    L_HTR = 3
    L_XTR = T - 1
    L_PROJ1 = T
    L_CHAIN1 = 2 * T
    L_GROW1 = 21
    L_CHAIN2 = 0
    L_GROW2 = 6
    L_P2 = 3 * T

    g1_rows = nc.dram_tensor("g1_rows", (H, N), F32).ap()
    g2_rows = nc.dram_tensor("g2_rows", (1, N), F32).ap()

    with ExitStack() as ctx:
        def sb(name, shape, dt=F32):
            return ctx.enter_context(nc.sbuf_tensor(name, shape, dt))

        def ps(name, shape, dt=F32):
            return ctx.enter_context(nc.psum_tensor(name, shape, dt))

        def sem(name):
            return ctx.enter_context(nc.semaphore(name))

        acc = [ps(f"acc{k}", [P, 512]) for k in range(4)]
        proj_ps = ps("proj_ps", [P, 512])
        xtr_ps = ps("xtr_ps", [P, 512])
        htr_ps = ps("htr_ps", [P, 512])
        misc_ps = ps("misc_ps", [P, 512])

        ident = sb("ident", [P, P])
        ident8 = sb("ident8", [P, P], U8)
        w1 = sb("w1", [P, KC, HF])
        w1ab = sb("w1ab", [P, KC, NA])
        w2 = sb("w2", [P, FC, V2W])
        bias1 = sb("bias1", [P, HF])
        bias2 = sb("bias2", [P, D])
        halfpow = sb("halfpow", [P, 1])
        eps_col = sb("eps_col", [P, 1])

        adj_t = [sb(f"adj{k}", [P, N], I32) for k in range(2)]
        mask = sb("mask", [P, 2, T, N], U8)
        p = sb("p", [P, 2, T, N])
        x_t = sb("x_t", [P, XR, D])
        xT = sb("xT", [P, 2, KC, P])
        v1 = sb("v1", [P, 2, T, H, VW])
        v2 = sb("v2", [P, 2, T, V2W])
        ab = sb("ab", [P, T, NA])
        amax = sb("amax", [P, H])
        A1 = sb("A1", [P, H])
        aC = sb("aC", [P, T, H])
        bC = sb("bC", [P, T, H])
        u1 = sb("u1", [P, 2, T, H])
        gcol1 = sb("gcol1", [P, H, T])
        grow1 = sb("grow1", [H * T, P])
        G1 = sb("G1", [P, H, N])
        amax2 = sb("amax2", [P, 1])
        A2 = sb("A2", [P, 1])
        aC2 = sb("aC2", [P, T])
        bC2 = sb("bC2", [P, T])
        u2 = sb("u2", [P, T])
        gcol2 = sb("gcol2", [P, T])
        grow2 = sb("grow2", [T, P])
        G2 = sb("G2", [P, N])
        rden = sb("rden", [P, 4])
        z = sb("z", [P, 4, P])
        e = sb("e", [P, 4, P])
        h = sb("h", [P, 4, P])
        hT = sb("hT", [P, H, N])
        y = sb("y", [P, XR, D])
        rden2 = sb("rden2", [P, 4])
        stats = sb("stats", [P, 4, 6])
        mv = sb("mv", [P, 4, 2])
        rstd = sb("rstd", [P, 4, 2])

        params_loaded = sem("params_loaded")
        ident_cleared = sem("ident_cleared")
        ident_ready = sem("ident_ready")
        ident8_ready = sem("ident8_ready")
        const_ready = sem("const_ready")
        fold_product = sem("fold_product")
        w_ready = sem("w_ready")
        adj_loaded = [sem(f"adj_loaded{k}") for k in range(2)]
        x_loaded = [sem(f"x_loaded{k}") for k in range(XR)]
        res_loaded = [sem(f"res_loaded{k}") for k in range(XR)]
        out_stored = [sem(f"out_stored{k}") for k in range(XR)]
        mask_compared = sem("mask_compared")
        mask_ready = sem("mask_ready")
        p1_ready = sem("p1_ready")
        p2_ready = sem("p2_ready")
        agg1_done = sem("agg1_done")
        agg2_done = sem("agg2_done")
        rden_ready = sem("rden_ready")
        z_ready = sem("z_ready")
        t_ready = sem("t_ready")
        e_ready = sem("e_ready")
        h_ready = sem("h_ready")
        htr_done = sem("htr_done")
        hT_ready = sem("hT_ready")
        xtr_done = sem("xtr_done")
        xT_ready = sem("xT_ready")
        proj1_done = sem("proj1_done")
        v1_raw = sem("v1_raw")
        proj2_done = sem("proj2_done")
        v2_raw = sem("v2_raw")
        ab_copied = sem("ab_copied")
        amax_ready = sem("amax_ready")
        A1_ready = sem("A1_ready")
        shifted1 = sem("shifted1")
        clamped1 = sem("clamped1")
        E1_ready = sem("E1_ready")
        u1_ready = sem("u1_ready")
        gcol1_ready = sem("gcol1_ready")
        grow1_turned = sem("grow1_turned")
        grow1_ready = sem("grow1_ready")
        g1_stored = sem("g1_stored")
        G1_loaded = sem("G1_loaded")
        v1_scaled = sem("v1_scaled")
        amax2_ready = sem("amax2_ready")
        A2_ready = sem("A2_ready")
        shifted2 = sem("shifted2")
        clamped2 = sem("clamped2")
        E2_ready = sem("E2_ready")
        u2_ready = sem("u2_ready")
        gcol2_ready = sem("gcol2_ready")
        grow2_turned = sem("grow2_turned")
        grow2_ready = sem("grow2_ready")
        g2_stored = sem("g2_stored")
        G2_loaded = sem("G2_loaded")
        v2_scaled = sem("v2_scaled")
        res_biased = sem("res_biased")
        rden2_ready = sem("rden2_ready")
        y_summed = sem("y_summed")
        stats_ready = sem("stats_ready")
        mv_ready = sem("mv_ready")
        var_ready = sem("var_ready")
        rstd_ready = sem("rstd_ready")
        y_ready = sem("y_ready")

        held = sem("held")

        def hold(engine, semaphore, value):
            engine.wait_ge(semaphore, value)
            engine.sem_inc(held, 1)

        def has(i):
            if isinstance(i, int):
                return 0 <= i < B, i >= 1, i < B - 1
            return True, True, True

        def first(i, n):
            return isinstance(i, int) and i < n

        def run(engine, body):
            body(-1, 1)
            body(0, 0)
            with engine.Fori(1, B - 2, 2) as i:
                body(i, 1)
                body(i + 1, 0)
            body(B - 1, 1)
            body(B, 0)

        block = ctx.enter_context(nc.Block())

        @block.sync
        def _(sp):
            sp.sem_inc(y_summed, T)
            sp.sem_inc(agg2_done, T)
            for k in range(XR):
                sp.sem_inc(out_stored[k], 16)
            for dst, src in (
                (w1[:], W1.rearrange("(c p) n -> p c n", p=P)),
                (w2[:, :, 0:D], W2.rearrange("(c p) n -> p c n", p=P)),
                (p[:, 0, 0, 0:HF], att_src1.rearrange("h f -> (h f)").partition_broadcast(P)),
                (p[:, 0, 0, HF:2 * HF], att_dst1.rearrange("h f -> (h f)").partition_broadcast(P)),
                (p[:, 0, 1, 0:D], att_src2.rearrange("h f -> (h f)").partition_broadcast(P)),
                (p[:, 0, 1, D:2 * D], att_dst2.rearrange("h f -> (h f)").partition_broadcast(P)),
                (bias1[:], b1.partition_broadcast(P)),
                (bias2[:], b2.partition_broadcast(P)),
            ):
                sp.dma_start(dst, src).then_inc(params_loaded, 16)

            def load_x(b, n, i):
                if not first(i, 0) or n >= XR:
                    hold(sp, xtr_done, b * T + n - XR + 1)
                sp.dma_start(x_t[:, n % XR, :], x[b, n * P:(n + 1) * P, :]).then_inc(x_loaded[n % XR], 16)

            def load_adj(b, s, i):
                if not first(i, 0) or s >= 2:
                    hold(sp, mask_ready, b * T + s - 1)
                sp.dma_start(adj_t[s % 2][:], adj[b, s * P:(s + 1) * P, :]).then_inc(adj_loaded[s % 2], 16)

            def load_residual(b, d, i):
                hold(sp, out_stored[d % XR], 16 * (2 * b + d // XR + 1))
                sp.dma_start(y[:, d % XR, :], x[b, d * P:(d + 1) * P, :]).then_inc(res_loaded[d % XR], 16)

            def store_y(b, d):
                hold(sp, y_ready, b * T + d + 1)
                sp.dma_start(out[b, d * P:(d + 1) * P, :], y[:, d % XR, :]).then_inc(out_stored[d % XR], 16)

            def body(i, par):
                l1, l2, nxt = has(i)
                for L in range(SLOTS + 2):
                    if nxt and L == 0:
                        for s in range(2):
                            load_adj(i + 1, s, i)
                        for n in range(XR):
                            load_x(i + 1, n, i)
                    if nxt and 0 <= L - L_XTR - 1 < T - XR:
                        load_x(i + 1, L - L_XTR - 1 + XR, i)
                    if l2 and L == L_GROW2 + 2:
                        hold(sp, grow2_ready, i)
                        sp.dma_start(g2_rows.rearrange("a (t c) -> (a t) c", c=P), grow2[:]).then_inc(g2_stored, 16)
                        hold(sp, g2_stored, 16 * i)
                        sp.dma_start(G2[:], g2_rows[0].partition_broadcast(P)).then_inc(G2_loaded, 16)
                    if nxt and L == L_GROW1 + 3:
                        hold(sp, grow1_ready, i + 2)
                        sp.dma_start(g1_rows.rearrange("h (t c) -> (h t) c", c=P), grow1[:]).then_inc(g1_stored, 16)
                        hold(sp, g1_stored, 16 * (i + 2))
                        if l1:
                            hold(sp, p1_ready, S1 * (i + 1))
                        sp.dma_start(G1[:].rearrange("p h n -> p (h n)"),
                                     g1_rows.rearrange("h n -> (h n)").partition_broadcast(P)).then_inc(G1_loaded, 16)
                    if l2 and L in range(L_P2 + 3, L_P2 + 3 + XR):
                        load_residual(i - 1, L - L_P2 - 3, i)
                    if nxt and S1 <= L and L - S1 + 2 < T:
                        load_adj(i + 1, L - S1 + 2, i)
                    d = L - S1 - 2
                    if l2 and 0 <= d < T:
                        if d >= 1 and d - 1 + XR < T:
                            load_residual(i - 1, d - 1 + XR, i)
                        store_y(i - 1, d)

            run(sp, body)
            for k in range(XR):
                sp.wait_ge(out_stored[k], 16 * (B * T // XR + 1))

        @block.tensor
        def _(pe):
            def transpose_x(b, n, i):
                pe.wait_ge(x_loaded[n % XR], 16 * (2 * b + n // XR + 1))
                if not first(i, 0) or n >= 1:
                    pe.wait_ge(xT_ready, b * T + n)
                for c in range(KC):
                    last = nc.tensor.transpose(xtr_ps[:, c * P:(c + 1) * P], x_t[:, n % XR, c * P:(c + 1) * P], ident[:])
                last.then_inc(xtr_done, 1)

            def project1(b, n, i):
                pe.wait_ge(xT_ready, b * T + n + 1)
                if n == 0:
                    if not first(i, 1):
                        pe.wait_ge(v2_raw, i * T)
                    if not first(i, 0):
                        pe.wait_ge(grow1_ready, i + 1)
                    if has(i)[1]:
                        pe.wait_ge(grow2_ready, i)
                else:
                    pe.wait_ge(v1_raw, b * T + n)
                for c in range(KC):
                    nc.tensor.matmul(misc_ps[:, n * NA:(n + 1) * NA], xT[:, n % 2, c, :], w1ab[:, c, :],
                                     start=(c == 0), stop=(c == KC - 1))
                for c in range(KC):
                    last = nc.tensor.matmul(proj_ps[:, 0:HF], xT[:, n % 2, c, :], w1[:, c, :],
                                            start=(c == 0), stop=(c == KC - 1))
                last.then_inc(proj1_done, 1)

            def transpose_h(i, m):
                pe.wait_ge(h_ready, i * S1 + m + 1)
                if not first(i, 1) or m >= 1:
                    pe.wait_ge(hT_ready, i * S1 + m)
                nc.tensor.transpose(htr_ps[:, 0:P], h[:, m % 4, :], ident[:]).then_inc(htr_done, 1)

            def project2(i, n):
                pe.wait_ge(hT_ready, i * S1 + (H - 1) * T + n + 1)
                if n >= 1:
                    pe.wait_ge(v2_raw, i * T + n)
                elif has(i)[2]:
                    pe.wait_ge(v1_raw, (i + 2) * T)
                else:
                    pe.wait_ge(v2_raw, i * T)
                for c in range(FC):
                    last = nc.tensor.matmul(proj_ps[:, 0:V2W], hT[:, c, n * P:(n + 1) * P], w2[:, c, :],
                                            start=(c == 0), stop=(c == FC - 1))
                last.then_inc(proj2_done, 1)

            def aggregate1(i, par, u, d):
                m = u * T + d
                if m >= 4:
                    pe.wait_ge(z_ready, i * S1 + m - 3)
                elif not first(i, 1):
                    pe.wait_ge(y_summed, i * T + m - 3)
                for s in range(T):
                    if d == 0:
                        if u == 0:
                            pe.wait_ge(v1_scaled, i * T + s + 1)
                        pe.wait_ge(p1_ready, i * S1 + m + s + 1)
                    last = nc.tensor.matmul(acc[d % 4][:, 0:VW], p[:, (par + u) % 2, s, d * P:(d + 1) * P],
                                            v1[:, par, s, u, :], start=(s == 0), stop=(s == T - 1))
                last.then_inc(agg1_done, 1)

            def aggregate2(i, par, d):
                if d >= 4:
                    pe.wait_ge(y_summed, i * T + d - 3)
                elif has(i)[0]:
                    pe.wait_ge(z_ready, i * S1 + S1 + d - 3)
                else:
                    pe.wait_ge(y_summed, i * T + d - 3)
                for s in range(T):
                    if d == 0:
                        pe.wait_ge(v2_scaled, (i - 1) * T + s + 1)
                        pe.wait_ge(p2_ready, (i - 1) * T + s + 1)
                    last = nc.tensor.matmul(acc[d % 4][:, 0:D + 1], p[:, par, s, d * P:(d + 1) * P],
                                            v2[:, 1 - par, s, 0:D + 1], start=(s == 0), stop=(s == T - 1))
                last.then_inc(agg2_done, 1)

            def body(i, par):
                l1, l2, nxt = has(i)
                for L in range(SLOTS):
                    if l1 and L < S1:
                        aggregate1(i, par, L // T, L % T)
                    if l2 and L >= S1:
                        aggregate2(i, par, L - S1)
                    if l2 and L == L_GROW2:
                        pe.wait_ge(gcol2_ready, i)
                        if l1:
                            pe.wait_ge(grow1_ready, i + 1)
                        nc.tensor.transpose(misc_ps[0:T, P:2 * P], gcol2[:], ident[:]).then_inc(grow2_turned, 1)
                    if nxt and 0 <= L - L_PROJ1 < T:
                        project1(i + 1, L - L_PROJ1, i)
                    if nxt and 0 <= L - L_XTR < T:
                        transpose_x(i + 1, L - L_XTR, i)
                    if nxt and L == L_GROW1:
                        pe.wait_ge(gcol1_ready, i + 2)
                        nc.tensor.transpose(misc_ps[0:H * T, P:2 * P], gcol1[:].rearrange("p h t -> p (h t)"),
                                            ident[:]).then_inc(grow1_turned, 1)
                    if l1 and 0 <= L - L_HTR < S1:
                        transpose_h(i, L - L_HTR)
                    if l1 and L >= S1:
                        project2(i, L - S1)

            pe.wait_ge(ident_ready, 1)
            pe.wait_ge(w_ready, 1)
            run(pe, body)

        @block.scalar
        def _(act):
            def elu_exp(i, m):
                act.wait_ge(z_ready, i * S1 + m + 1)
                if not first(i, 1) or m >= 4:
                    act.wait_ge(h_ready, i * S1 + m - 3)
                nc.scalar.activation(e[:, m % 4, :], z[:, m % 4, :], ACT.Relu, scale=-1.0).then_inc(t_ready, 1)
                act.wait_ge(t_ready, i * S1 + m + 1)
                nc.scalar.activation(e[:, m % 4, :], e[:, m % 4, :], ACT.Exp, scale=-1.0).then_inc(e_ready, 1)

            def copy_xT(b, n, i):
                act.wait_ge(xtr_done, b * T + n + 1)
                if not first(i, 0) or n >= 2:
                    act.wait_ge(proj1_done, b * T + n - 1)
                nc.scalar.copy(xT[:, n % 2, :, :].rearrange("p c n -> p (c n)"), xtr_ps[:, 0:KC * P]).then_inc(xT_ready, 1)

            def copy_v1(b, n, par, i):
                act.wait_ge(proj1_done, b * T + n + 1)
                if n == 0 and not first(i, 1):
                    act.wait_ge(agg1_done, i * S1)
                nc.scalar.copy(v1[:, 1 - par, n, :, 0:F], proj_ps[:, 0:HF].rearrange("p (h f) -> p h f", h=H)).then_inc(v1_raw, 1)

            def copy_hT(i, m):
                act.wait_ge(htr_done, i * S1 + m + 1)
                if m == 0 and not first(i, 1):
                    act.wait_ge(proj2_done, i * T)
                nc.scalar.copy(hT[:, m // T, (m % T) * P:(m % T + 1) * P], htr_ps[:, 0:P]).then_inc(hT_ready, 1)

            def copy_v2(i, par, n):
                act.wait_ge(proj2_done, i * T + n + 1)
                if n == 0 and not first(i, 1):
                    act.wait_ge(agg2_done, i * T)
                nc.scalar.copy(v2[:, par, n, :], proj_ps[:, 0:V2W]).then_inc(v2_raw, 1)

            def body(i, par):
                l1, l2, nxt = has(i)
                for L in range(SLOTS + 1):
                    if l1 and 1 <= L <= S1:
                        elu_exp(i, L - 1)
                    if l2 and L == L_CHAIN2 + 4:
                        act.wait_ge(clamped2, 2 * i)
                        nc.scalar.activation(gcol2[:], bC2[:], ACT.Exp, scale=GAP).then_inc(gcol2_ready, 1)
                        nc.scalar.activation(v2[:, 1 - par, :, D], aC2[:], ACT.Exp).then_inc(E2_ready, 1)
                        nc.scalar.activation(u2[:], aC2[:], ACT.Exp, scale=-GAP).then_inc(u2_ready, 1)
                    if l2 and L == L_GROW2 + 1:
                        act.wait_ge(grow2_turned, i)
                        nc.scalar.copy(grow2[:], misc_ps[0:T, P:2 * P]).then_inc(grow2_ready, 1)
                    if nxt and 1 <= L - L_XTR <= T:
                        copy_xT(i + 1, L - L_XTR - 1, i)
                    if nxt and 1 <= L - L_PROJ1 <= T:
                        copy_v1(i + 1, L - L_PROJ1 - 1, par, i)
                    if nxt and L == L_CHAIN1 + 4:
                        act.wait_ge(clamped1, 2 * (i + 2))
                        nc.scalar.activation(gcol1[:], bC[:].rearrange("p t h -> p h t"), ACT.Exp, scale=GAP).then_inc(gcol1_ready, 1)
                        nc.scalar.activation(u1[:, 1 - par, :, :], aC[:], ACT.Exp, scale=-GAP).then_inc(u1_ready, 1)
                        nc.scalar.activation(v1[:, 1 - par, :, :, F], aC[:], ACT.Exp).then_inc(E1_ready, 1)
                    if nxt and L == L_GROW1 + 1:
                        act.wait_ge(grow1_turned, i + 2)
                        if not first(i, 0):
                            act.wait_ge(g1_stored, 16 * (i + 1))
                        nc.scalar.copy(grow1[:], misc_ps[0:H * T, P:2 * P]).then_inc(grow1_ready, 1)
                    if l1 and 1 <= L - L_HTR <= S1:
                        copy_hT(i, L - L_HTR - 1)
                    if l1 and L > S1:
                        copy_v2(i, par, L - S1 - 1)

            act.wait_ge(w_ready, 1)
            run(act, body)

        @block.gpsimd
        def _(pool):
            nc.gpsimd.memset(halfpow[:], -0.5).then_inc(const_ready, 1)
            nc.gpsimd.memset(eps_col[:], EPS).then_inc(const_ready, 1)
            nc.gpsimd.memset(ident[:], 0.0).then_inc(ident_cleared, 1)
            pool.wait_ge(ident_cleared, 1)
            nc.gpsimd.affine_select(out=ident[:], in_=ident[:], compare_op=ALU.not_equal, fill=1.0, base=0,
                                    pattern=[[-1, P]], channel_multiplier=1).then_inc(ident_ready, 1)
            pool.wait_ge(const_ready, 2)
            pool.wait_ge(params_loaded, 16 * 8)

            def scale_v1(b, n, par):
                v = v1[:, par, n, :, 0:F]
                E = v1[:, par, n, :, F:F + 1].broadcast_to([P, H, F])
                nc.gpsimd.tensor_tensor(v, v, E, ALU.mult).then_inc(v1_scaled, 1)

            def scale_v2(n, par):
                v = v2[:, par, n, 0:D]
                nc.gpsimd.tensor_tensor(v, v, v2[:, par, n, D:D + 1].broadcast_to([P, D]), ALU.mult).then_inc(v2_scaled, 1)

            def bias_residual(b, d):
                pool.wait_ge(res_loaded[d % XR], 16 * (2 * b + d // XR + 1))
                nc.gpsimd.tensor_tensor(y[:, d % XR, :], y[:, d % XR, :], bias2[:], ALU.add).then_inc(res_biased, 1)

            def inverse_deviation(b, d):
                pool.wait_ge(mv_ready, b * T + d + 1)
                nc.gpsimd.tensor_tensor(rstd[:, d % 4, 0:1], mv[:, d % 4, 1:2], eps_col[:], ALU.add).then_inc(var_ready, 1)
                pool.wait_ge(var_ready, b * T + d + 1)
                nc.gpsimd.tensor_tensor(rstd[:, d % 4, 1:2], rstd[:, d % 4, 0:1], halfpow[:], ALU.pow).then_inc(rstd_ready, 1)

            def body(i, par):
                l1, l2, nxt = has(i)
                for L in range(SLOTS + 3):
                    if l2 and L == L_CHAIN2 + 1:
                        hold(pool, amax2_ready, i)
                        nc.gpsimd.partition_all_reduce(A2[:], amax2[:], P, RMAX).then_inc(A2_ready, 1)
                    if l2 and 5 <= L - L_CHAIN2 < 5 + T:
                        if L == L_CHAIN2 + 5:
                            pool.wait_ge(E2_ready, i)
                        scale_v2(L - L_CHAIN2 - 5, 1 - par)
                    if nxt and L == L_CHAIN1 + 2:
                        hold(pool, amax_ready, i + 2)
                        nc.gpsimd.partition_all_reduce(A1[:], amax[:], P, RMAX).then_inc(A1_ready, 1)
                    if nxt and 5 <= L - L_CHAIN1 < 5 + T:
                        if L == L_CHAIN1 + 5:
                            pool.wait_ge(E1_ready, i + 2)
                            pool.wait_ge(v1_raw, (i + 2) * T)
                        scale_v1(i + 1, L - L_CHAIN1 - 5, 1 - par)
                    if l2 and 0 <= L - (S1 + 2) < T:
                        inverse_deviation(i - 1, L - (S1 + 2))
                    if l2 and 0 <= L - (S1 - 1) < T:
                        bias_residual(i - 1, L - (S1 - 1))

            run(pool, body)

        @block.vector
        def _(dve):
            dve.wait_ge(ident_ready, 1)
            nc.vector.tensor_copy(ident8[:], ident[:]).then_inc(ident8_ready, 1)
            dve.wait_ge(params_loaded, 16 * 8)
            folds = [(w1[:, c, q * F:(q + 1) * F], p[:, 0, 0, (g * H + q) * F:(g * H + q + 1) * F],
                      w1ab[:, c, g * H + q:g * H + q + 1]) for c in range(KC) for g in range(2) for q in range(H)]
            folds += [(w2[:, c, 0:D], p[:, 0, 1, g * D:(g + 1) * D], w2[:, c, D + g:D + g + 1])
                      for c in range(FC) for g in range(2)]
            for n, (w, a, dst) in enumerate(folds):
                k = w.shape[-1]
                if n >= 1:
                    dve.wait_ge(fold_product, n)
                ins = nc.vector.tensor_tensor_reduce(p[:, 0, 2, 0:k], w, a, 1.0, 0.0, ALU.mult, ALU.add, dst)
                ins.then_inc(fold_product, 1)
            dve.wait_ge(fold_product, len(folds))
            nc.vector.memset(rden[:], 0.0).then_inc(w_ready, 1)
            dve.wait_ge(w_ready, 1)
            dve.wait_ge(ident8_ready, 1)

            def make_mask(b, par, s):
                dve.wait_ge(adj_loaded[s % 2], 16 * (4 * b + s // 2 + 1))
                nc.vector.tensor_scalar(mask[:, par, s, :], adj_t[s % 2][:], 0.0, None, ALU.is_gt).then_inc(mask_compared, 1)
                dve.wait_ge(mask_compared, b * T + s + 1)
                own = mask[:, par, s, s * P:(s + 1) * P]
                nc.vector.tensor_tensor(own, own, ident8[:], ALU.max).then_inc(mask_ready, 1)

            def weights1(b, par, u, s):
                if u == 0:
                    dve.wait_ge(mask_ready, b * T + s + 1)
                    if s == 0:
                        dve.wait_ge(G1_loaded, 16 * (b + 1))
                        dve.wait_ge(u1_ready, b + 1)
                nc.vector.scalar_tensor_tensor(out=p[:, (par + u) % 2, s, :], in0=G1[:, u, :], scalar=u1[:, par, s, u:u + 1],
                                               in1=mask[:, par, s, :], op0=ALU.max, op1=ALU.mult).then_inc(p1_ready, 1)

            def weights2(i, par, s):
                if s == 0:
                    dve.wait_ge(G2_loaded, 16 * i)
                    dve.wait_ge(u2_ready, i)
                nc.vector.scalar_tensor_tensor(out=p[:, par, s, :], in0=G2[:], scalar=u2[:, s:s + 1],
                                               in1=mask[:, 1 - par, s, :], op0=ALU.max, op1=ALU.mult).then_inc(p2_ready, 1)

            def normalise1(i, m):
                dve.wait_ge(agg1_done, i * S1 + m + 1)
                if not first(i, 1) or m >= 4:
                    dve.wait_ge(h_ready, i * S1 + m - 3)
                nc.vector.reciprocal(rden[:, m % 4:m % 4 + 1], acc[m % 4][:, F:F + 1]).then_inc(rden_ready, 1)
                dve.wait_ge(rden_ready, i * S1 + m + 1)
                nc.vector.scalar_tensor_tensor(out=z[:, m % 4, :], in0=acc[m % 4][:, 0:F], scalar=rden[:, m % 4:m % 4 + 1],
                                               in1=bias1[:, (m // T) * F:(m // T + 1) * F], op0=ALU.mult, op1=ALU.add).then_inc(z_ready, 1)

            def elu(i, m):
                dve.wait_ge(e_ready, i * S1 + m + 1)
                if not first(i, 1) or m >= 4:
                    dve.wait_ge(htr_done, i * S1 + m - 3)
                nc.vector.scalar_tensor_tensor(out=h[:, m % 4, :], in0=e[:, m % 4, :], scalar=-1.0,
                                               in1=z[:, m % 4, :], op0=ALU.add, op1=ALU.max).then_inc(h_ready, 1)

            def residual(i, d):
                q = (i - 1) * T + d + 1
                dve.wait_ge(agg2_done, i * T + d + 1)
                if d >= 4 or not has(i)[0]:
                    dve.wait_ge(y_ready, q - 4)
                nc.vector.reciprocal(rden2[:, d % 4:d % 4 + 1], acc[d % 4][:, D:D + 1]).then_inc(rden2_ready, 1)
                dve.wait_ge(rden2_ready, q)
                dve.wait_ge(res_biased, q)
                nc.vector.scalar_tensor_tensor(out=y[:, d % XR, :], in0=acc[d % 4][:, 0:D], scalar=rden2[:, d % 4:d % 4 + 1],
                                               in1=y[:, d % XR, :], op0=ALU.mult, op1=ALU.add).then_inc(y_summed, 1)
                dve.wait_ge(y_summed, q + T)
                nc.vector.bn_stats(stats[:, d % 4, :], y[:, d % XR, :]).then_inc(stats_ready, 1)
                hold(dve, stats_ready, q)
                nc.vector.bn_aggr(mv[:, d % 4, :], stats[:, d % 4, :]).then_inc(mv_ready, 1)

            def layer_norm(i, d):
                dve.wait_ge(rstd_ready, (i - 1) * T + d + 1)
                nc.vector.tensor_scalar(y[:, d % XR, :], y[:, d % XR, :], mv[:, d % 4, 0:1], rstd[:, d % 4, 1:2],
                                        ALU.subtract, ALU.mult).then_inc(y_ready, 1)

            def factors1(i, par, L):
                k = i + 2
                a, b = ab[:, :, 0:H], ab[:, :, H:NA]
                if L == 0:
                    dve.wait_ge(proj1_done, k * T)
                    nc.vector.tensor_copy(ab[:].rearrange("p t j -> p (t j)"), misc_ps[:, 0:T * NA]).then_inc(ab_copied, 1)
                    dve.wait_ge(ab_copied, k)
                    nc.vector.tensor_reduce(amax[:], a.rearrange("p t h -> p h t"), AX.X, ALU.max).then_inc(amax_ready, 1)
                if L == 3:
                    dve.wait_ge(A1_ready, k)
                    A = A1[:].unsqueeze(1).broadcast_to([P, T, H])
                    if not first(i, 0):
                        dve.wait_ge(E1_ready, k - 1)
                    nc.vector.tensor_tensor(bC[:], b, A, ALU.add).then_inc(shifted1, 1)
                    nc.vector.tensor_tensor(aC[:], a, A, ALU.subtract).then_inc(shifted1, 1)
                    dve.wait_ge(shifted1, 2 * k)
                    nc.vector.tensor_scalar(bC[:], bC[:], RANGE, None, ALU.min).then_inc(clamped1, 1)
                    nc.vector.tensor_scalar(aC[:], aC[:], -RANGE, None, ALU.max).then_inc(clamped1, 1)

            def factors2(i, par, L):
                a, b = v2[:, 1 - par, :, D], v2[:, 1 - par, :, D + 1]
                if L == 0:
                    dve.wait_ge(v2_raw, i * T)
                    nc.vector.tensor_reduce(amax2[:], a, AX.X, ALU.max).then_inc(amax2_ready, 1)
                if L == 3:
                    dve.wait_ge(A2_ready, i)
                    nc.vector.tensor_scalar(bC2[:], b, A2[:, 0:1], RANGE, ALU.add, ALU.min).then_inc(clamped2, 1)
                    nc.vector.tensor_scalar(aC2[:], a, A2[:, 0:1], -RANGE, ALU.subtract, ALU.max).then_inc(clamped2, 1)

            def body(i, par):
                l1, l2, nxt = has(i)
                for L in range(SLOTS + 3):
                    u, s = L // T, L % T
                    if l1 and 1 <= L <= S1:
                        normalise1(i, L - 1)
                    if l2 and 1 <= L - S1 <= T:
                        residual(i, L - S1 - 1)
                    if l1 and 2 <= L <= S1 + 1:
                        elu(i, L - 2)
                    if nxt and u == H:
                        make_mask(i + 1, 1 - par, s)
                    if l1 and u < H - 1:
                        if s == 0 and u == 0 and not first(i, 1):
                            dve.wait_ge(agg2_done, i * T)
                        if s == 0 and u > 0:
                            dve.wait_ge(agg1_done, i * S1 + u * T)
                        weights1(i, par, u + 1, s)
                    if l2 and u == H - 1:
                        if s == 0 and l1:
                            dve.wait_ge(agg1_done, i * S1 + u * T)
                        weights2(i, par, s)
                    if nxt and u == H:
                        if s == 0 and l1:
                            dve.wait_ge(agg1_done, (i + 1) * S1)
                        weights1(i + 1, 1 - par, 0, s)
                    if nxt:
                        factors1(i, par, L - L_CHAIN1)
                    if l2:
                        factors2(i, par, L - L_CHAIN2)
                    if l2 and 3 <= L - S1 < 3 + T:
                        layer_norm(i, L - S1 - 3)

            run(dve, body)


_INS = ["x", "adj", "L0_gnn_W1", "L0_gnn_att_src1", "L0_gnn_att_dst1", "L0_gnn_b1", "L0_gnn_W2", "L0_gnn_att_src2",
        "L0_gnn_att_dst2", "L0_gnn_b2"]
_OUTS = [((8, 1024, 256), "float32")]


def kernel(**inputs):
    import numpy as _np
    import concourse.bacc as _bacc
    from concourse import mybir as _mybir
    from concourse.bass_utils import run_bass_kernel_spmd as _run

    nc = _bacc.Bacc("TRN2", target_bir_lowering=False, num_devices=1)
    arrays, args = {}, []
    for name in _INS:
        a = _np.ascontiguousarray(inputs[name])
        arrays[f"in_{name}_dram"] = a
        args.append(nc.dram_tensor(f"in_{name}_dram", a.shape, _mybir.dt.from_np(a.dtype), kind="ExternalInput").ap())
    for i, (shape, dtype) in enumerate(_OUTS):
        dt = _mybir.dt.from_np(_np.dtype(dtype))
        args.append(nc.dram_tensor(f"out_{i}_dram", shape, dt, kind="ExternalOutput").ap())
    build_gat(nc, *args)
    r = _run(nc, [arrays], core_ids=[0])
    got = tuple(r.results[0][f"out_{i}_dram"] for i in range(len(_OUTS)))
    return got[0]
```

```python
from contextlib import ExitStack

import concourse.bass as bass
from concourse import mybir

ALU = mybir.AluOpType
ACT = mybir.ActivationFunctionType
AX = mybir.AxisListType
F32 = mybir.dt.float32
F16 = mybir.dt.float16
I32 = mybir.dt.int32
U8 = mybir.dt.uint8
RMAX = bass.bass_isa.ReduceOp.max

P = 128
SLOPE = 0.2
GAP = 1.0 - SLOPE
RANGE = 86.0
SPLIT_RANGE = 7.0
SPLIT_SPREAD = 6.0
SPLIT_LARGE = 6e4
SPLIT_SMALL = 16.0
G_FLOOR = -0.85
HI_FACTOR = 1.0 - 2.0 ** -11 - 2.0 ** -20
VSCALE = 256.0
EPS = 1e-5
XR = 4
UNITS = 5


def build_gat(nc, x, adj, W1, att_src1, att_dst1, b1, W2, att_src2, att_dst2, b2, out):
    B, N, D = x.shape
    H, F = att_src1.shape
    HF = H * F
    T = N // P
    KC = D // P
    FC = HF // P
    VW = F + 2
    V2W = D + 2
    S1 = H * T
    SLOTS = UNITS * T
    NA = 2 * H
    GB = 4
    GROUPS = S1 // GB
    assert F == P and T == 8 and KC == 2

    htr_slot = [min(m + 3, S1 + 1) for m in range(S1)]
    elu_slot = [htr_slot[m + 3] + 1 for m in range(0, S1, 4)]
    L_PROJ1 = (9, 11, 12, 14, 15, 17, 18, 20)
    L_CHAIN1 = 21
    L_GROW1 = 27
    L_CHAIN2 = 0
    L_GROW2 = 7
    L_HIGH2 = 6
    L_LOW2 = 16
    L_P2 = 3 * T

    g1_rows = nc.dram_tensor("g1_rows", (H, N), F32).ap()
    g2_rows = nc.dram_tensor("g2_rows", (1, N), F32).ap()

    with ExitStack() as ctx:
        def sb(name, shape, dt=F32):
            return ctx.enter_context(nc.sbuf_tensor(name, shape, dt))

        def ps(name, shape, dt=F32):
            return ctx.enter_context(nc.psum_tensor(name, shape, dt))


        acc = [ps(f"acc{k}", [P, 512]) for k in range(4)]
        proj_ps = ps("proj_ps", [P, 512])
        xtr_ps = ps("xtr_ps", [P, 512])
        htr_ps = ps("htr_ps", [P, 512])
        misc_ps = ps("misc_ps", [P, 512])

        ident = sb("ident", [P, P])
        ident8 = sb("ident8", [P, P], U8)
        w1 = sb("w1", [P, KC, HF])
        w1ab = sb("w1ab", [P, KC, NA])
        w2 = sb("w2", [P, FC, V2W])
        bias1 = sb("bias1", [P, H])
        bias2 = sb("bias2", [P, D])
        halfpow = sb("halfpow", [P, 1])
        minus_one = sb("minus_one", [P, 1])

        adj_t = [sb(f"adj{k}", [P, N], I32) for k in range(2)]
        mask = sb("mask", [P, 2, T, N], U8)
        mask2 = sb("mask2", [P, T, N], U8)
        p = sb("p", [P, 2, T, N])
        x_t = sb("x_t", [P, XR, D])
        xT = sb("xT", [P, 2, KC, P])
        raw1 = sb("raw1", [P, T, HF])
        raw2 = sb("raw2", [P, T, V2W])
        v1 = sb("v1", [P, T, H, VW])
        v2 = sb("v2", [P, T, V2W])
        v1s = v1[:].rearrange("p t h v -> p (t h v)").bitcast(F16).rearrange("p (t h k v) -> p t h k v", t=T, h=H, k=2)
        v2s = v2[:].rearrange("p t v -> p (t v)").bitcast(F16).rearrange("p (t k v) -> p t k v", t=T, k=2)
        p_pair = p[:].rearrange("p b t n -> p (b t n)").bitcast(F16).rearrange("p (b t n k) -> p b t n k", b=2, t=T, k=2)
        ab = sb("ab", [P, T, NA])
        amax = sb("amax", [P, H])
        A1 = sb("A1", [P, H])
        aC = sb("aC", [P, T, H])
        bC = sb("bC", [P, T, H])
        ug1 = sb("ug1", [P, 2, 2, H * T])
        exp1 = sb("exp1", [P, 2, H * T])
        exp2 = sb("exp2", [P, 2, T])
        E1 = sb("E1", [P, T, H])
        E2 = sb("E2", [P, T])
        grow1 = sb("grow1", [H * T, P])
        G1 = sb("G1", [P, 2, N])
        amax2 = sb("amax2", [P, 1])
        A2 = sb("A2", [P, 1])
        aC2 = sb("aC2", [P, T])
        bC2 = sb("bC2", [P, T])
        ug2 = sb("ug2", [P, 2, T])
        grow2 = sb("grow2", [T, P])
        G2 = sb("G2", [P, N])
        den = sb("den", [P, 4])
        rden = sb("rden", [P, 4])
        z0 = sb("z0", [P, 4, P])
        z = sb("z", [P, GB * P])
        e = sb("e", [P, GB * P])
        hT = sb("hT", [P, H, N])
        y = sb("y", [P, XR, D])
        rden2 = sb("rden2", [P, 4])
        squares = sb("squares", [P, HF], F16)
        norms = sb("norms", [P, 2, T])
        extremes = sb("extremes", [P, 2, 2])
        bounds = sb("bounds", [P, 3, 2])
        bounds_all = sb("bounds_all", [P, 3, 2])
        within = sb("within", [P, 6])
        verdict = sb("verdict", [P, 1], I32)
        stats = sb("stats", [P, 4, 6])
        mv = sb("mv", [P, 4, 2])
        rstd = sb("rstd", [P, 4, 2])

        def one_pass(split, pass_ctx, semaphores):
            def sem(name):
                semaphores.append(nc.alloc_semaphore(f"{name}_{'split' if split else 'general'}"))
                return semaphores[-1]

            params1_loaded = sem("params1_loaded")
            params2_loaded = sem("params2_loaded")
            ident_cleared = sem("ident_cleared")
            ident_ready = sem("ident_ready")
            ident8_ready = sem("ident8_ready")
            const_ready = sem("const_ready")
            fold_product = sem("fold_product")
            fold2_product = sem("fold2_product")
            w1_ready = sem("w1_ready")
            w2_ready = sem("w2_ready")
            adj_loaded = [sem(f"adj_loaded{k}") for k in range(2)]
            x_loaded = [sem(f"x_loaded{k}") for k in range(XR)]
            res_loaded = [sem(f"res_loaded{k}") for k in range(XR)]
            out_stored = [sem(f"out_stored{k}") for k in range(XR)]
            mask_compared = sem("mask_compared")
            mask_ready = sem("mask_ready")
            p1_ready = sem("p1_ready")
            p2_ready = sem("p2_ready")
            agg1_done = sem("agg1_done")
            agg2_done = sem("agg2_done")
            den_copied = sem("den_copied")
            rden_ready = sem("rden_ready")
            z0_ready = sem("z0_ready")
            z_ready = sem("z_ready")
            t_ready = sem("t_ready")
            e_ready = sem("e_ready")
            htr_done = sem("htr_done")
            hT_ready = sem("hT_ready")
            xtr_done = sem("xtr_done")
            xT_ready = sem("xT_ready")
            proj1_done = sem("proj1_done")
            v1_raw = sem("v1_raw")
            proj2_done = sem("proj2_done")
            v2_raw = sem("v2_raw")
            ab_copied = sem("ab_copied")
            amax_ready = sem("amax_ready")
            A1_ready = sem("A1_ready")
            shifted1 = sem("shifted1")
            clamped1 = sem("clamped1")
            E1_ready = sem("E1_ready")
            exp1_ready = sem("exp1_ready")
            hi1_packed = sem("hi1_packed")
            ug1_ready = sem("ug1_ready")
            grow1_turned = sem("grow1_turned")
            grow1_ready = sem("grow1_ready")
            g1_stored = sem("g1_stored")
            G1_loaded = [sem(f"G1_loaded{q}") for q in range(2)]
            mask_copied = sem("mask_copied")
            v1_hi = sem("v1_hi")
            v1_lo = sem("v1_lo")
            bounds1_taken = sem("bounds1_taken")
            bounds2_taken = sem("bounds2_taken")
            bounds_ready = sem("bounds_ready")
            bounds_reduced = sem("bounds_reduced")
            compared = sem("compared")
            amax2_ready = sem("amax2_ready")
            A2_ready = sem("A2_ready")
            shifted2 = sem("shifted2")
            clamped2 = sem("clamped2")
            E2_ready = sem("E2_ready")
            exp2_ready = sem("exp2_ready")
            hi2_packed = sem("hi2_packed")
            ug2_ready = sem("ug2_ready")
            grow2_turned = sem("grow2_turned")
            grow2_ready = sem("grow2_ready")
            g2_stored = sem("g2_stored")
            G2_loaded = sem("G2_loaded")
            v2_hi = sem("v2_hi")
            v2_lo = sem("v2_lo")
            v1_ready, v2_ready = (v1_lo, v2_lo) if split else (v1_hi, v2_hi)
            res_biased = sem("res_biased")
            rden2_ready = sem("rden2_ready")
            y_summed = sem("y_summed")
            stats_ready = sem("stats_ready")
            mv_ready = sem("mv_ready")
            var_ready = sem("var_ready")
            rstd_ready = sem("rstd_ready")
            y_ready = sem("y_ready")

            held = sem("held")

            def hold(engine, semaphore, value):
                engine.wait_ge(semaphore, value)
                engine.sem_inc(held, 1)

            reach = SPLIT_RANGE if split else RANGE

            def has(i):
                if isinstance(i, int):
                    return 0 <= i < B, i >= 1, i < B - 1
                return True, True, True

            def first(i, n):
                return isinstance(i, int) and i < n

            def proj1_slot(i, n):
                return (n + 2, n) if first(i, 0) else (L_PROJ1[n], L_PROJ1[n] - 2)

            def mask_slot(i, s):
                return s + 1 if first(i, 0) else L_PROJ1[s]

            def run(engine, body):
                body(-1, 1)
                body(0, 0)
                with engine.Fori(1, B - 2, 2) as i:
                    body(i, 1)
                    body(i + 1, 0)
                body(B - 1, 1)
                body(B, 0)

            def when_needed(engine, program):
                if split:
                    program()
                else:
                    in_bounds = engine.value_load(verdict[0:1, 0:1], min_val=0, max_val=1)
                    with engine.If(in_bounds == 0):
                        program()

            block = pass_ctx.enter_context(nc.Block())

            @block.sync
            def _(sp):
                def load_x(b, n, i):
                    if not first(i, 0) or n >= XR:
                        hold(sp, xtr_done, b * T + n - XR + 1)
                    sp.dma_start(x_t[:, n % XR, :], x[b, n * P:(n + 1) * P, :]).then_inc(x_loaded[n % XR], 16)

                def load_adj(b, s, i):
                    if not first(i, 0) or s >= 2:
                        hold(sp, mask_ready, b * T + s - 1)
                    sp.dma_start(adj_t[s % 2][:], adj[b, s * P:(s + 1) * P, :]).then_inc(adj_loaded[s % 2], 16)

                def load_G1(b, q):
                    sp.dma_start(G1[:, q % 2, :], g1_rows[q].partition_broadcast(P)).then_inc(G1_loaded[q % 2], 16)

                def load_residual(b, d, i):
                    hold(sp, out_stored[d % XR], 16 * (2 * b + d // XR + 1))
                    sp.dma_start(y[:, d % XR, :], x[b, d * P:(d + 1) * P, :]).then_inc(res_loaded[d % XR], 16)

                def store_y(b, d):
                    hold(sp, y_ready, b * T + d + 1)
                    sp.dma_start(out[b, d * P:(d + 1) * P, :], y[:, d % XR, :]).then_inc(out_stored[d % XR], 16)

                def body(i, par):
                    l1, l2, nxt = has(i)
                    for L in range(SLOTS + 2):
                        if l1 and L in (0, T):
                            q = 2 + L // T
                            hold(sp, p1_ready, i * S1 + (q - 1) * T)
                            load_G1(i, q)
                        if l1 and L == S1:
                            hold(sp, p1_ready, S1 * (i + 1))
                            if l2:
                                hold(sp, p2_ready, i * T)
                            sp.dma_start(mask2[:], mask[:, par, :, :]).then_inc(mask_copied, 16)
                        if nxt and L == 0 and not first(i, 0):
                            for s in range(2):
                                load_adj(i + 1, s, i)
                            for n in range(XR):
                                load_x(i + 1, n, i)
                        for n in range(XR, T):
                            if nxt and L == proj1_slot(i, n - XR)[1] + 1:
                                load_x(i + 1, n, i)
                        if l2 and L == L_GROW2 + 2:
                            hold(sp, grow2_ready, i)
                            sp.dma_start(g2_rows.rearrange("a (t c) -> (a t) c", c=P), grow2[:]).then_inc(g2_stored, 16)
                            hold(sp, g2_stored, 16 * i)
                            sp.dma_start(G2[:], g2_rows[0].partition_broadcast(P)).then_inc(G2_loaded, 16)
                        if nxt and L == L_GROW1 + 1:
                            if l1:
                                hold(sp, p1_ready, S1 * (i + 1))
                            hold(sp, grow1_ready, i + 2)
                            sp.dma_start(g1_rows.rearrange("h (t c) -> (h t) c", c=P), grow1[:]).then_inc(g1_stored, 16)
                            hold(sp, g1_stored, 16 * (i + 2))
                            for q in range(2):
                                load_G1(i + 1, q)
                        if l2 and L in range(L_P2 + 3, L_P2 + 3 + XR):
                            load_residual(i - 1, L - L_P2 - 3, i)
                        for s in range(2, T):
                            if nxt and L == mask_slot(i, s - 2):
                                load_adj(i + 1, s, i)
                        d = L - S1 - 2
                        if l2 and 0 <= d < T:
                            if d >= 1 and d - 1 + XR < T:
                                load_residual(i - 1, d - 1 + XR, i)
                            store_y(i - 1, d)

                def start():
                    sp.sem_inc(y_summed, T)
                    sp.sem_inc(agg2_done, T)
                    for k in range(XR):
                        sp.sem_inc(out_stored[k], 16)
                    for n in range(XR):
                        load_x(0, n, -1)
                    if split:
                        for dst, src in (
                            (w1[:], W1.rearrange("(c p) n -> p c n", p=P)),
                            (p[:, 0, 0, 0:HF], att_src1.rearrange("h f -> (h f)").partition_broadcast(P)),
                            (p[:, 0, 0, HF:2 * HF], att_dst1.rearrange("h f -> (h f)").partition_broadcast(P)),
                        ):
                            sp.dma_start(dst, src).then_inc(params1_loaded, 16)
                    for s in range(2):
                        load_adj(0, s, -1)
                    if split:
                        for dst, src in (
                            (w2[:, :, 0:D], W2.rearrange("(c p) n -> p c n", p=P)),
                            (p[:, 1, 0, 0:D], att_src2.rearrange("h f -> (h f)").partition_broadcast(P)),
                            (p[:, 1, 0, D:2 * D], att_dst2.rearrange("h f -> (h f)").partition_broadcast(P)),
                            (bias2[:], b2.partition_broadcast(P)),
                        ):
                            sp.dma_start(dst, src).then_inc(params2_loaded, 16)
                        sp.dma_start(bias1[:], b1.rearrange("(h f) -> f h", f=F),
                                     allow_slow_non_contiguous=True).then_inc(params2_loaded, 16)

                def program():
                    start()
                    run(sp, body)
                    for k in range(XR):
                        sp.wait_ge(out_stored[k], 16 * (B * T // XR + 1))

                when_needed(sp, program)

            @block.tensor
            def _(pe):
                def transpose_x(b, n, i):
                    pe.wait_ge(x_loaded[n % XR], 16 * (2 * b + n // XR + 1))
                    if not first(i, 0) or n >= 1:
                        pe.wait_ge(xT_ready, b * T + n)
                    for c in range(KC):
                        last = nc.tensor.transpose(xtr_ps[:, c * P:(c + 1) * P], x_t[:, n % XR, c * P:(c + 1) * P], ident[:])
                    last.then_inc(xtr_done, 1)

                def project1(b, n, i):
                    pe.wait_ge(xT_ready, b * T + n + 1)
                    dst = acc[n % 4] if first(i, 0) else proj_ps
                    if first(i, 0):
                        if n == 0 and split:
                            pe.wait_ge(w1_ready, 1)
                        if n >= 4:
                            pe.wait_ge(v1_raw, b * T + n - 3)
                    elif n == 0:
                        if not first(i, 1):
                            pe.wait_ge(v2_raw, i * T)
                        pe.wait_ge(grow1_ready, i + 1)
                        if has(i)[1]:
                            pe.wait_ge(grow2_ready, i)
                    else:
                        pe.wait_ge(v1_raw, b * T + n)
                    for c in range(KC):
                        nc.tensor.matmul(misc_ps[:, n * NA:(n + 1) * NA], xT[:, n % 2, c, :], w1ab[:, c, :],
                                         start=(c == 0), stop=(c == KC - 1))
                    for c in range(KC):
                        last = nc.tensor.matmul(dst[:, 0:HF], xT[:, n % 2, c, :], w1[:, c, :],
                                                start=(c == 0), stop=(c == KC - 1))
                    last.then_inc(proj1_done, 1)

                def transpose_h(i, m):
                    pe.wait_ge(z0_ready, i * S1 + m + 1)
                    if m % GB == 0 and (not first(i, 1) or m >= 1):
                        pe.wait_ge(z_ready, i * GROUPS + m // GB)
                    nc.tensor.transpose(htr_ps[:, (m % GB) * P:(m % GB + 1) * P], z0[:, m % 4, :], ident[:]).then_inc(htr_done, 1)

                def project2(i, n):
                    if split and n == 0 and first(i, 1):
                        pe.wait_ge(w2_ready, 1)
                    if n % GB == 0:
                        pe.wait_ge(hT_ready, i * GROUPS + ((H - 1) * T + n) // GB + 1)
                    if n >= 1:
                        pe.wait_ge(v2_raw, i * T + n)
                    elif has(i)[2]:
                        pe.wait_ge(v1_raw, (i + 2) * T)
                    else:
                        pe.wait_ge(v2_raw, i * T)
                    for c in range(FC):
                        last = nc.tensor.matmul(proj_ps[:, 0:V2W], hT[:, c, n * P:(n + 1) * P], w2[:, c, :],
                                                start=(c == 0), stop=(c == FC - 1))
                    last.then_inc(proj2_done, 1)

                def products(dst, buf, s, d, v, v_hi, v_lo):
                    block = slice(d * P, (d + 1) * P)
                    if not split:
                        return nc.tensor.matmul(dst, p[:, buf, s, block], v, start=(s == 0), stop=(s == T - 1))
                    p_hi, p_lo = p_pair[:, buf, s, block, 1], p_pair[:, buf, s, block, 0]
                    nc.tensor.matmul(dst, p_hi, v_lo, start=(s == 0), stop=False)
                    nc.tensor.matmul(dst, p_hi, v_hi, start=False, stop=False)
                    return nc.tensor.matmul(dst, p_lo, v_hi, start=False, stop=(s == T - 1))

                def aggregate1(i, par, u, d):
                    m = u * T + d
                    if m >= 4:
                        pe.wait_ge(z0_ready, i * S1 + m - 3)
                    elif not first(i, 1):
                        pe.wait_ge(y_summed, i * T + m - 3)
                    for s in range(T):
                        if d == 0:
                            if u == 0:
                                pe.wait_ge(v1_ready, i * T + s + 1)
                            pe.wait_ge(p1_ready, i * S1 + m + s + 1)
                        last = products(acc[d % 4][:, 0:F + 1], (par + u) % 2, s, d, v1[:, s, u, 0:F + 1],
                                        v1s[:, s, u, 0, 0:F + 1], v1s[:, s, u, 1, 0:F + 1])
                    last.then_inc(agg1_done, 1)

                def aggregate2(i, par, d):
                    if d >= 4:
                        pe.wait_ge(y_summed, i * T + d - 3)
                    elif has(i)[0]:
                        pe.wait_ge(z0_ready, i * S1 + S1 + d - 3)
                    else:
                        pe.wait_ge(y_summed, i * T + d - 3)
                    for s in range(T):
                        if d == 0:
                            pe.wait_ge(v2_ready, (i - 1) * T + s + 1)
                            pe.wait_ge(p2_ready, (i - 1) * T + s + 1)
                        last = products(acc[d % 4][:, 0:D + 1], par, s, d, v2[:, s, 0:D + 1],
                                        v2s[:, s, 0, 0:D + 1], v2s[:, s, 1, 0:D + 1])
                    last.then_inc(agg2_done, 1)

                def body(i, par):
                    l1, l2, nxt = has(i)
                    for L in range(SLOTS):
                        if l1 and L < S1:
                            aggregate1(i, par, L // T, L % T)
                        if l2 and L >= S1:
                            aggregate2(i, par, L - S1)
                        if l2 and L == L_GROW2:
                            pe.wait_ge(ug2_ready, i)
                            if l1:
                                pe.wait_ge(grow1_ready, i + 1)
                            nc.tensor.transpose(misc_ps[0:T, P:2 * P], ug2[:, 1, :], ident[:]).then_inc(grow2_turned, 1)
                        for n in range(T):
                            if nxt and L == proj1_slot(i, n)[0]:
                                project1(i + 1, n, i)
                        for n in range(T):
                            if nxt and L == proj1_slot(i, n)[1]:
                                transpose_x(i + 1, n, i)
                        if nxt and L == L_GROW1:
                            pe.wait_ge(ug1_ready, i + 2)
                            nc.tensor.transpose(misc_ps[0:H * T, P:2 * P], ug1[:, 1 - par, 1, :],
                                                ident[:]).then_inc(grow1_turned, 1)
                        for m in range(S1):
                            if l1 and L == htr_slot[m]:
                                transpose_h(i, m)
                        if l1 and L >= S1:
                            project2(i, L - S1)

                def program():
                    if split:
                        pe.wait_ge(ident_ready, 1)
                    run(pe, body)

                when_needed(pe, program)

            @block.scalar
            def _(act):
                def copy_den1(i, m):
                    act.wait_ge(agg1_done, i * S1 + m + 1)
                    nc.scalar.copy(den[:, m % 4:m % 4 + 1], acc[m % 4][:, F:F + 1]).then_inc(den_copied, 1)

                def normalise1(i, m):
                    act.wait_ge(rden_ready, i * S1 + m + 1)
                    if not first(i, 1) or m >= 4:
                        act.wait_ge(htr_done, i * S1 + m - 3)
                    nc.scalar.activation(z0[:, m % 4, :], acc[m % 4][:, 0:F], ACT.Copy,
                                         scale=rden[:, m % 4:m % 4 + 1]).then_inc(z0_ready, 1)

                def elu_exp(i, g):
                    q = g * GB // T
                    act.wait_ge(htr_done, i * S1 + (g + 1) * GB)
                    if not first(i, 1) or g >= 1:
                        act.wait_ge(hT_ready, i * GROUPS + g)
                    elif split:
                        act.wait_ge(params2_loaded, 16 * 5)
                    nc.scalar.activation(z[:], htr_ps[:], ACT.Identity, bias=bias1[:, q:q + 1]).then_inc(z_ready, 1)
                    act.wait_ge(z_ready, i * GROUPS + g + 1)
                    nc.scalar.activation(e[:], z[:], ACT.Relu, scale=-1.0).then_inc(t_ready, 1)
                    act.wait_ge(t_ready, i * GROUPS + g + 1)
                    nc.scalar.activation(e[:], e[:], ACT.Exp, scale=-1.0).then_inc(e_ready, 1)

                def copy_xT(b, n, i):
                    act.wait_ge(xtr_done, b * T + n + 1)
                    if not first(i, 0) or n >= 2:
                        act.wait_ge(proj1_done, b * T + n - 1)
                    nc.scalar.copy(xT[:, n % 2, :, :].rearrange("p c n -> p (c n)"), xtr_ps[:, 0:KC * P]).then_inc(xT_ready, 1)

                def copy_raw1(b, n, i):
                    act.wait_ge(proj1_done, b * T + n + 1)
                    src = acc[n % 4] if first(i, 0) else proj_ps
                    if n == 0 and not first(i, 0):
                        act.wait_ge(v1_ready, b * T)
                    if split:
                        if not first(i, 0) or n >= 1:
                            act.wait_ge(v1_raw, b * T + n)
                        nc.scalar.activation(squares[:], src[:, 0:HF], ACT.Square, accum_out=norms[:, 0, n:n + 1])
                    nc.scalar.mul(raw1[:, n, :], src[:, 0:HF], VSCALE).then_inc(v1_raw, 1)

                def finish_v1(b, n, l1):
                    if n == 0:
                        act.wait_ge(E1_ready, b + 1)
                        act.wait_ge(v1_raw, (b + 1) * T)
                        if l1:
                            act.wait_ge(agg1_done, b * S1)
                        nc.scalar.mul(v1s[:, :, :, 0, F] if split else v1[:, :, :, F], E1[:], VSCALE)
                    dst = v1s[:, n, :, 0, 0:F] if split else v1[:, n, :, 0:F]
                    for q in range(H):
                        last = nc.scalar.activation(dst[:, q, :], raw1[:, n, q * F:(q + 1) * F], ACT.Copy, scale=E1[:, n, q:q + 1])
                    last.then_inc(v1_hi, 1)

                def finish_v2(i, n):
                    if n == 0:
                        act.wait_ge(E2_ready, i)
                        act.wait_ge(v2_raw, i * T)
                        act.wait_ge(agg2_done, i * T)
                        nc.scalar.mul(v2s[:, :, 0, D] if split else v2[:, :, D], E2[:], VSCALE)
                    dst = v2s[:, n, 0, 0:D] if split else v2[:, n, 0:D]
                    nc.scalar.activation(dst, raw2[:, n, 0:D], ACT.Copy, scale=E2[:, n:n + 1]).then_inc(v2_hi, 1)

                def copy_raw2(i, n):
                    act.wait_ge(proj2_done, i * T + n + 1)
                    if n == 0 and not first(i, 1):
                        act.wait_ge(v2_ready, i * T)
                    if split:
                        nc.scalar.activation(squares[:, 0:D], proj_ps[:, 0:D], ACT.Square, accum_out=norms[:, 1, n:n + 1])
                    nc.scalar.mul(raw2[:, n, :], proj_ps[:, 0:V2W], VSCALE).then_inc(v2_raw, 1)

                def body(i, par):
                    l1, l2, nxt = has(i)
                    for L in range(SLOTS + 1):
                        if l1 and 1 <= L <= S1:
                            copy_den1(i, L - 1)
                        for n in range(T):
                            if nxt and L == proj1_slot(i, n)[1] + 1:
                                copy_xT(i + 1, n, i)
                        for n in range(T):
                            if nxt and L == proj1_slot(i, n)[0] + 1:
                                copy_raw1(i + 1, n, i)
                        if l1 and S1 < L <= SLOTS:
                            copy_raw2(i, L - S1 - 1)
                        if l1 and 2 <= L <= S1 + 1:
                            normalise1(i, L - 2)
                        if l2 and L == L_CHAIN2 + 4:
                            act.wait_ge(clamped2, i)
                            nc.scalar.activation(E2[:], aC2[:], ACT.Exp).then_inc(E2_ready, 1)
                            nc.scalar.activation(exp2[:, 1, :], bC2[:], ACT.Exp, scale=GAP).then_inc(exp2_ready, 1)
                            nc.scalar.activation(exp2[:, 0, :], aC2[:], ACT.Exp, scale=-GAP).then_inc(exp2_ready, 1)
                        if l2 and L == L_GROW2 + 1:
                            act.wait_ge(grow2_turned, i)
                            nc.scalar.copy(grow2[:], misc_ps[0:T, P:2 * P]).then_inc(grow2_ready, 1)
                        if nxt and L == L_CHAIN1 + 4:
                            act.wait_ge(clamped1, 2 * (i + 2))
                            nc.scalar.activation(E1[:], aC[:], ACT.Exp).then_inc(E1_ready, 1)
                            nc.scalar.activation(exp1[:, 1, :].rearrange("p (h t) -> p h t", h=H),
                                                 bC[:].rearrange("p t h -> p h t"), ACT.Exp, scale=GAP).then_inc(exp1_ready, 1)
                            nc.scalar.activation(exp1[:, 0, :].rearrange("p (t h) -> p t h", h=H),
                                                 aC[:], ACT.Exp, scale=-GAP).then_inc(exp1_ready, 1)
                        if nxt and L == L_GROW1 + 1:
                            act.wait_ge(grow1_turned, i + 2)
                            if not first(i, 0):
                                act.wait_ge(g1_stored, 16 * (i + 1))
                            nc.scalar.copy(grow1[:], misc_ps[0:H * T, P:2 * P]).then_inc(grow1_ready, 1)
                        if l1 and L in elu_slot:
                            elu_exp(i, elu_slot.index(L))
                        if l2 and 0 <= L - L_HIGH2 < T:
                            finish_v2(i, L - L_HIGH2)
                        if nxt and 0 <= L - S1 < T:
                            finish_v1(i + 1, L - S1, l1)

                def program():
                    run(act, body)

                when_needed(act, program)

            @block.gpsimd
            def _(pool):
                def invert1(i, m):
                    pool.wait_ge(den_copied, i * S1 + m + 1)
                    nc.gpsimd.tensor_tensor(rden[:, m % 4:m % 4 + 1], den[:, m % 4:m % 4 + 1], minus_one[:],
                                            ALU.pow).then_inc(rden_ready, 1)

                def inverse_deviation(b, d):
                    pool.wait_ge(var_ready, b * T + d + 1)
                    nc.gpsimd.tensor_tensor(rstd[:, d % 4, 1:2], rstd[:, d % 4, 0:1], halfpow[:], ALU.pow).then_inc(rstd_ready, 1)

                def bias_residual(b, d):
                    pool.wait_ge(res_loaded[d % XR], 16 * (2 * b + d // XR + 1))
                    nc.gpsimd.tensor_tensor(y[:, d % XR, :], y[:, d % XR, :], bias2[:], ALU.add).then_inc(res_biased, 1)

                def body(i, par):
                    l1, l2, nxt = has(i)
                    for L in range(SLOTS + 1):
                        if l1 and 1 <= L <= S1:
                            invert1(i, L - 1)
                        if l2 and L == L_CHAIN2 + 1:
                            hold(pool, amax2_ready, i)
                            nc.gpsimd.partition_all_reduce(A2[:], amax2[:], P, RMAX).then_inc(A2_ready, 1)
                        if nxt and L == L_CHAIN1 + 2:
                            hold(pool, amax_ready, i + 2)
                            nc.gpsimd.partition_all_reduce(A1[:], amax[:], P, RMAX).then_inc(A1_ready, 1)
                        if l2 and 1 <= L - S1 <= T:
                            inverse_deviation(i - 1, L - S1 - 1)
                        if l2 and 0 <= L - (S1 - 1) < T:
                            bias_residual(i - 1, L - (S1 - 1))

                def start():
                    nc.gpsimd.memset(halfpow[:], -0.5).then_inc(const_ready, 1)
                    nc.gpsimd.memset(minus_one[:], -1.0).then_inc(const_ready, 1)
                    nc.gpsimd.memset(ident[:], 0.0).then_inc(ident_cleared, 1)
                    pool.wait_ge(ident_cleared, 1)
                    nc.gpsimd.affine_select(out=ident[:], in_=ident[:], compare_op=ALU.not_equal, fill=1.0, base=0,
                                            pattern=[[-1, P]], channel_multiplier=1).then_inc(ident_ready, 1)
                    pool.wait_ge(const_ready, 2)
                    pool.wait_ge(params2_loaded, 16 * 5)

                def program():
                    if split:
                        start()
                    run(pool, body)
                    if split:
                        pool.wait_ge(bounds_ready, 1)
                        nc.gpsimd.partition_all_reduce(bounds_all[:].rearrange("p k l -> p (k l)"),
                                                       bounds[:].rearrange("p k l -> p (k l)"), P, RMAX).then_inc(bounds_reduced, 1)

                when_needed(pool, program)

            @block.vector
            def _(dve):
                def make_mask(b, par, s):
                    if s == 0 and not first(b, 2):
                        dve.wait_ge(mask_copied, 16 * (b - 1))
                    dve.wait_ge(adj_loaded[s % 2], 16 * (4 * b + s // 2 + 1))
                    nc.vector.tensor_scalar(mask[:, par, s, :], adj_t[s % 2][:], 0.0, None, ALU.is_gt).then_inc(mask_compared, 1)
                    dve.wait_ge(mask_compared, b * T + s + 1)
                    own = mask[:, par, s, s * P:(s + 1) * P]
                    nc.vector.tensor_tensor(own, own, ident8[:], ALU.max).then_inc(mask_ready, 1)

                def weights1(b, par, u, s):
                    if u == 0:
                        dve.wait_ge(mask_ready, b * T + s + 1)
                    if s == 0:
                        dve.wait_ge(G1_loaded[u % 2], 16 * (2 * b + u // 2 + 1))
                    nc.vector.scalar_tensor_tensor(out=p[:, (par + u) % 2, s, :], in0=G1[:, u % 2, :], scalar=ug1[:, par, 0, s * H + u:s * H + u + 1],
                                                   in1=mask[:, par, s, :], op0=ALU.max, op1=ALU.mult).then_inc(p1_ready, 1)

                def weights2(i, par, s):
                    if s == 0:
                        dve.wait_ge(G2_loaded, 16 * i)
                        dve.wait_ge(mask_copied, 16 * i)
                    nc.vector.scalar_tensor_tensor(out=p[:, par, s, :], in0=G2[:], scalar=ug2[:, 0, s:s + 1],
                                                   in1=mask2[:, s, :], op0=ALU.max, op1=ALU.mult).then_inc(p2_ready, 1)

                def elu(i, g):
                    q, part = g * GB // T, g % (T // GB)
                    dve.wait_ge(e_ready, i * GROUPS + g + 1)
                    if g == 0 and not first(i, 1):
                        dve.wait_ge(proj2_done, i * T)
                    nc.vector.scalar_tensor_tensor(out=hT[:, q, part * GB * P:(part + 1) * GB * P], in0=e[:], scalar=-1.0,
                                                   in1=z[:], op0=ALU.add, op1=ALU.max).then_inc(hT_ready, 1)

                def invert2(i, d):
                    q = (i - 1) * T + d + 1
                    dve.wait_ge(agg2_done, i * T + d + 1)
                    nc.vector.reciprocal(rden2[:, d % 4:d % 4 + 1], acc[d % 4][:, D:D + 1]).then_inc(rden2_ready, 1)

                def residual(i, d):
                    q = (i - 1) * T + d + 1
                    dve.wait_ge(rden2_ready, q)
                    dve.wait_ge(res_biased, q)
                    nc.vector.scalar_tensor_tensor(out=y[:, d % XR, :], in0=acc[d % 4][:, 0:D], scalar=rden2[:, d % 4:d % 4 + 1],
                                                   in1=y[:, d % XR, :], op0=ALU.mult, op1=ALU.add).then_inc(y_summed, 1)

                def moments(i, d):
                    q = (i - 1) * T + d + 1
                    dve.wait_ge(y_summed, q + T)
                    nc.vector.bn_stats(stats[:, d % 4, :], y[:, d % XR, :]).then_inc(stats_ready, 1)
                    hold(dve, stats_ready, q)
                    nc.vector.bn_aggr(mv[:, d % 4, :], stats[:, d % 4, :]).then_inc(mv_ready, 1)
                    dve.wait_ge(mv_ready, q)
                    nc.vector.tensor_scalar(rstd[:, d % 4, 0:1], mv[:, d % 4, 1:2], EPS, None, ALU.add).then_inc(var_ready, 1)

                def layer_norm(i, d):
                    dve.wait_ge(rstd_ready, (i - 1) * T + d + 1)
                    nc.vector.tensor_scalar(y[:, d % XR, :], y[:, d % XR, :], mv[:, d % 4, 0:1], rstd[:, d % 4, 1:2],
                                            ALU.subtract, ALU.mult).then_inc(y_ready, 1)

                def take_bounds(taken, made, n, layer, a_least):
                    dve.wait_ge(taken, n * 5 + made)
                    nc.vector.tensor_reduce(extremes[:, layer, 0:1], norms[:, layer, :], AX.X, ALU.max).then_inc(taken, 1)
                    nc.vector.tensor_reduce(extremes[:, layer, 1:2], a_least, AX.X, ALU.min).then_inc(taken, 1)
                    dve.wait_ge(taken, n * 5 + made + 2)
                    for k, e_k, op in ((0, 0, ALU.max), (1, 0, ALU.min), (2, 1, ALU.min)):
                        bound = bounds[:, k, layer:layer + 1]
                        nc.vector.tensor_tensor(bound, bound, extremes[:, layer, e_k:e_k + 1], op).then_inc(taken, 1)

                def pack(word, value, hi_packed, ready, k):
                    if not split:
                        nc.vector.tensor_copy(word, value).then_inc(ready, 1)
                        return
                    pair = word.bitcast(F16).rearrange("p (n k) -> p n k", k=2)
                    nc.vector.tensor_scalar(pair[:, :, 1], value, HI_FACTOR, None, ALU.mult).then_inc(hi_packed, 1)
                    dve.wait_ge(hi_packed, k)
                    nc.vector.tensor_tensor(pair[:, :, 0], value, pair[:, :, 1], ALU.subtract).then_inc(ready, 1)

                def factors1(i, par, L):
                    k = i + 2
                    a, b = ab[:, :, 0:H], ab[:, :, H:NA]
                    if L == 0:
                        dve.wait_ge(proj1_done, k * T)
                        nc.vector.tensor_copy(ab[:].rearrange("p t j -> p (t j)"), misc_ps[:, 0:T * NA]).then_inc(ab_copied, 1)
                        dve.wait_ge(ab_copied, k)
                        nc.vector.tensor_reduce(amax[:], a.rearrange("p t h -> p h t"), AX.X, ALU.max).then_inc(amax_ready, 1)
                    if L == 3:
                        dve.wait_ge(A1_ready, k)
                        A = A1[:].unsqueeze(1).broadcast_to([P, T, H])
                        nc.vector.tensor_tensor(bC[:], b, A, ALU.add).then_inc(shifted1, 1)
                        nc.vector.tensor_tensor(aC[:], a, A, ALU.subtract).then_inc(shifted1, 1)
                        dve.wait_ge(shifted1, 2 * k)
                        if split:
                            dve.wait_ge(v1_raw, k * T)
                            take_bounds(bounds1_taken, 1, i + 1, 0, aC[:].rearrange("p t h -> p (t h)"))
                            dve.wait_ge(bounds1_taken, 5 * k + 1)
                        nc.vector.tensor_scalar(bC[:], bC[:], reach, G_FLOOR, ALU.min, ALU.max).then_inc(clamped1, 1)
                        nc.vector.tensor_scalar(aC[:], aC[:], -reach, None, ALU.max).then_inc(clamped1, 1)
                    if L == 5:
                        dve.wait_ge(exp1_ready, 2 * k)
                        pack(ug1[:, 1 - par, :, :].rearrange("p k n -> p (k n)"), exp1[:].rearrange("p k n -> p (k n)"),
                             hi1_packed, ug1_ready, k)

                def factors2(i, par, L):
                    a, b = raw2[:, :, D], raw2[:, :, D + 1]
                    if L == 0:
                        dve.wait_ge(v2_raw, i * T)
                        nc.vector.tensor_reduce(amax2[:], a, AX.X, ALU.max).then_inc(amax2_ready, 1)
                    if L == 3:
                        dve.wait_ge(A2_ready, i)
                        nc.vector.tensor_scalar(bC2[:], b, A2[:, 0:1], reach, ALU.add, ALU.min).then_inc(shifted2, 1)
                        nc.vector.tensor_scalar(aC2[:], a, A2[:, 0:1], -reach, ALU.subtract, ALU.max).then_inc(shifted2, 1)
                        dve.wait_ge(shifted2, 2 * i)
                        if split:
                            take_bounds(bounds2_taken, 2, i - 1, 1, aC2[:])
                        nc.vector.tensor_scalar(bC2[:], bC2[:], G_FLOOR, None, ALU.max).then_inc(clamped2, 1)
                    if L == 5:
                        dve.wait_ge(exp2_ready, 2 * i)
                        pack(ug2[:].rearrange("p k n -> p (k n)"), exp2[:].rearrange("p k n -> p (k n)"),
                             hi2_packed, ug2_ready, i)

                def low_part1(n, b):
                    dve.wait_ge(v1_hi, b * T + n + 1)
                    if n == 0:
                        nc.vector.scalar_tensor_tensor(out=v1s[:, :, :, 1, F], in0=E1[:], scalar=VSCALE,
                                                       in1=v1s[:, :, :, 0, F], op0=ALU.mult, op1=ALU.subtract)
                    for q in range(H):
                        last = nc.vector.scalar_tensor_tensor(out=v1s[:, n, q, 1, 0:F], in0=raw1[:, n, q * F:(q + 1) * F],
                                                              scalar=E1[:, n, q:q + 1], in1=v1s[:, n, q, 0, 0:F],
                                                              op0=ALU.mult, op1=ALU.subtract)
                    last.then_inc(v1_lo, 1)

                def low_part2(n, i):
                    dve.wait_ge(v2_hi, (i - 1) * T + n + 1)
                    if n == 0:
                        nc.vector.scalar_tensor_tensor(out=v2s[:, :, 1, D], in0=E2[:], scalar=VSCALE,
                                                       in1=v2s[:, :, 0, D], op0=ALU.mult, op1=ALU.subtract)
                    nc.vector.scalar_tensor_tensor(out=v2s[:, n, 1, 0:D], in0=raw2[:, n, 0:D], scalar=E2[:, n:n + 1],
                                                   in1=v2s[:, n, 0, 0:D], op0=ALU.mult, op1=ALU.subtract).then_inc(v2_lo, 1)

                def body(i, par):
                    l1, l2, nxt = has(i)
                    for L in range(SLOTS + 2):
                        u, s = L // T, L % T
                        for n in range(T):
                            if nxt and L == mask_slot(i, n):
                                make_mask(i + 1, 1 - par, n)
                        if split and first(i, 0) and L == mask_slot(i, T - 1) + 1:
                            fold2()
                        if l1 and u < H - 1:
                            if s == 0 and u == 0 and not first(i, 1):
                                dve.wait_ge(agg2_done, i * T)
                            if s == 0 and u > 0:
                                dve.wait_ge(agg1_done, i * S1 + u * T)
                            weights1(i, par, u + 1, s)
                        if l2 and u == H - 1:
                            if s == 0 and l1:
                                dve.wait_ge(agg1_done, i * S1 + u * T)
                            weights2(i, par, s)
                        if nxt and u == H:
                            if s == 0 and l1:
                                dve.wait_ge(agg1_done, (i + 1) * S1)
                            weights1(i + 1, 1 - par, 0, s)
                        if nxt:
                            factors1(i, par, L - L_CHAIN1)
                        if l2:
                            factors2(i, par, L - L_CHAIN2)
                        if l1 and L - 1 in elu_slot:
                            elu(i, elu_slot.index(L - 1))
                        if l2 and 1 <= L - S1 <= T:
                            invert2(i, L - S1 - 1)
                        if split and nxt and u == H:
                            low_part1(s, i + 1)
                        if l2 and 1 <= L - S1 <= T:
                            residual(i, L - S1 - 1)
                        if l2 and 2 <= L - S1 <= T + 1:
                            layer_norm(i, L - S1 - 2)
                        if l2 and 1 <= L - S1 <= T:
                            moments(i, L - S1 - 1)
                        if split and l2 and 0 <= L - L_LOW2 < T:
                            low_part2(L - L_LOW2, i)

                def fold(folds, products, product_ready):
                    for n, (w, a, dst, factor) in enumerate(folds):
                        k = w.shape[-1]
                        if n >= 1:
                            dve.wait_ge(product_ready, n)
                        nc.vector.tensor_tensor_reduce(products[:, 0:k], w, a, factor, 0.0, ALU.mult, ALU.add,
                                                       dst).then_inc(product_ready, 1)
                    dve.wait_ge(product_ready, len(folds))

                def fold2():
                    dve.wait_ge(params2_loaded, 16 * 5)
                    fold([(w2[:, c, 0:D], p[:, 1, 0, g * D:(g + 1) * D], w2[:, c, D + g:D + g + 1], 1.0 / VSCALE)
                          for c in range(FC) for g in range(2)], p[:, 1, 1, :], fold2_product)
                    nc.vector.memset(rden2[:], 0.0).then_inc(w2_ready, 1)
                    dve.wait_ge(w2_ready, 1)

                def start():
                    dve.wait_ge(ident_ready, 1)
                    nc.vector.tensor_copy(ident8[:], ident[:]).then_inc(ident8_ready, 1)
                    dve.wait_ge(ident8_ready, 1)
                    dve.wait_ge(params1_loaded, 16 * 3)
                    folds = [(w1[:, c, q * F:(q + 1) * F], p[:, 0, 0, (g * H + q) * F:(g * H + q + 1) * F],
                              w1ab[:, c, g * H + q:g * H + q + 1], 1.0) for c in range(KC) for g in range(2) for q in range(H)]
                    fold(folds, p[:, 0, 1, :], fold_product)
                    nc.vector.memset(rden[:], 0.0).then_inc(w1_ready, 1)
                    dve.wait_ge(w1_ready, 1)
                    nc.vector.memset(bounds[:, 0, :], 0.0).then_inc(bounds1_taken, 1)
                    nc.vector.memset(bounds[:, 1, :], SPLIT_LARGE).then_inc(bounds2_taken, 1)
                    nc.vector.memset(bounds[:, 2, :], 0.0).then_inc(bounds2_taken, 1)
                    dve.wait_ge(bounds2_taken, 2)

                def judge():
                    dve.wait_ge(bounds1_taken, 5 * B + 1)
                    dve.wait_ge(bounds2_taken, 5 * B + 2)
                    least = bounds[:, 1:3, :].rearrange("p k l -> p (k l)")
                    nc.vector.tensor_scalar(least, least, -1.0, None, ALU.mult).then_inc(bounds_ready, 1)
                    dve.wait_ge(bounds_reduced, 1)
                    for k, limit in enumerate((SPLIT_LARGE, -SPLIT_SMALL, SPLIT_SPREAD)):
                        nc.vector.tensor_scalar(within[:, 2 * k:2 * k + 2], bounds_all[:, k, :], limit, None,
                                                ALU.is_le).then_inc(compared, 1)
                    dve.wait_ge(compared, 3)
                    nc.vector.tensor_reduce(verdict[:], within[:], AX.X, ALU.min)

                def program():
                    if split:
                        start()
                    run(dve, body)
                    if split:
                        judge()

                when_needed(dve, program)

        for split in (True, False):
            semaphores = []
            with ExitStack() as pass_ctx:
                one_pass(split, pass_ctx, semaphores)
            nc.clear_and_free_semaphores(semaphores)
            nc.all_engine_barrier()


_INS = ["x", "adj", "L0_gnn_W1", "L0_gnn_att_src1", "L0_gnn_att_dst1", "L0_gnn_b1", "L0_gnn_W2", "L0_gnn_att_src2",
        "L0_gnn_att_dst2", "L0_gnn_b2"]
_OUTS = [((8, 1024, 256), "float32")]


def kernel(**inputs):
    import numpy as _np
    import concourse.bacc as _bacc
    from concourse import mybir as _mybir
    from concourse.bass_utils import run_bass_kernel_spmd as _run

    nc = _bacc.Bacc("TRN2", target_bir_lowering=False, num_devices=1)
    arrays, args = {}, []
    for name in _INS:
        a = _np.ascontiguousarray(inputs[name])
        arrays[f"in_{name}_dram"] = a
        args.append(nc.dram_tensor(f"in_{name}_dram", a.shape, _mybir.dt.from_np(a.dtype), kind="ExternalInput").ap())
    for i, (shape, dtype) in enumerate(_OUTS):
        dt = _mybir.dt.from_np(_np.dtype(dtype))
        args.append(nc.dram_tensor(f"out_{i}_dram", shape, dt, kind="ExternalOutput").ap())
    build_gat(nc, *args)
    r = _run(nc, [arrays], core_ids=[0])
    got = tuple(r.results[0][f"out_{i}_dram"] for i in range(len(_OUTS)))
    return got[0]
```

```python
from contextlib import ExitStack

import concourse.bass as bass
from concourse import mybir

ALU = mybir.AluOpType
ACT = mybir.ActivationFunctionType
AX = mybir.AxisListType
F32 = mybir.dt.float32
F32R = mybir.dt.float32r
F16 = mybir.dt.float16
I32 = mybir.dt.int32
U8 = mybir.dt.uint8
RMAX = bass.bass_isa.ReduceOp.max

P = 128
SLOPE = 0.2
GAP = 1.0 - SLOPE
RANGE = 86.0
SPLIT_RANGE = 7.0
SPLIT_SPREAD = 6.0
SPLIT_LARGE = 6e4
SPLIT_SMALL = 16.0
G_FLOOR = -0.85
HI_FACTOR = 1.0 - 2.0 ** -11 - 2.0 ** -20
VSCALE = 256.0
EPS = 1e-5
XR = 4
UNITS = 5


def build_gat(nc, x, adj, W1, att_src1, att_dst1, b1, W2, att_src2, att_dst2, b2, out):
    B, N, D = x.shape
    H, F = att_src1.shape
    HF = H * F
    T = N // P
    KC = D // P
    FC = HF // P
    VW = F + 2
    V2W = D + 2
    S1 = H * T
    SLOTS = UNITS * T
    NA = 2 * H
    GB = 4
    GROUPS = S1 // GB
    assert F == P and T == 8 and KC == 2

    htr_slot = [min(m + 3, S1 + 1) for m in range(S1)]
    elu_slot = [htr_slot[m + 3] + 1 for m in range(0, S1, 4)]
    L_PROJ1 = (9, 11, 12, 14, 15, 17, 18, 20)
    L_CHAIN1 = 21
    L_GROW1 = 28
    L_FOLD2 = T
    L_CHAIN2 = 0
    L_GROW2 = 7
    L_JUDGE = 9
    L_HIGH2 = 6
    L_LOW2 = 16
    L_P2 = 3 * T

    g1_rows = nc.dram_tensor("g1_rows", (H, N), F32).ap()
    g2_rows = nc.dram_tensor("g2_rows", (1, N), F32).ap()

    with ExitStack() as ctx:
        def sb(name, shape, dt=F32):
            return ctx.enter_context(nc.sbuf_tensor(name, shape, dt))

        def ps(name, shape, dt=F32):
            return ctx.enter_context(nc.psum_tensor(name, shape, dt))

        acc = [ps(f"acc{k}", [P, 512]) for k in range(4)]
        proj_ps = ps("proj_ps", [P, 512])
        xtr_ps = ps("xtr_ps", [P, 512])
        htr_ps = ps("htr_ps", [P, 512])
        misc_ps = ps("misc_ps", [P, 512])

        ident = sb("ident", [P, P])
        WA = HF // 2 + NA
        w1 = sb("w1", [P, 2, KC, HF + NA], F32R)
        w2 = sb("w2", [P, FC, V2W])
        bias1 = sb("bias1", [P, H])
        bias2 = sb("bias2", [P, D])
        halfpow = sb("halfpow", [P, 1])
        minus_one = sb("minus_one", [P, 1])

        adj_t = [sb(f"adj{k}", [P, N], I32) for k in range(2)]
        mask = sb("mask", [P, 2, T, N], U8)
        mask2 = sb("mask2", [P, T, N], U8)
        p = sb("p", [P, 2, T, N])
        x_t = sb("x_t", [P, XR, D])
        xT = sb("xT", [P, 2, 2, KC, P], F32R)
        raw1 = sb("raw1", [P, T, HF])
        raw2 = sb("raw2", [P, T, V2W])
        hT = sb("hT", [P, H, N])
        v1 = sb("v1", [P, T, H, VW])
        v2 = sb("v2", [P, T, V2W])
        w1_whole = hT[:].rearrange("p h n -> p (h n)")[:, 0:KC * (HF + NA)].rearrange("p (c n) -> p c n", c=KC)
        att2 = raw2[:].rearrange("p t v -> p (t v)")
        v1s = v1[:].rearrange("p t h v -> p (t h v)").bitcast(F16).rearrange("p (t h k v) -> p t h k v", t=T, h=H, k=2)
        v2s = v2[:].rearrange("p t v -> p (t v)").bitcast(F16).rearrange("p (t k v) -> p t k v", t=T, k=2)
        p_pair = p[:].rearrange("p b t n -> p (b t n)").bitcast(F16).rearrange("p (b t n k) -> p b t n k", b=2, t=T, k=2)
        ab = sb("ab", [P, T, NA])
        amax = sb("amax", [P, H])
        A1 = sb("A1", [P, H])
        aC = sb("aC", [P, T, H])
        bC = sb("bC", [P, T, H])
        ug1 = sb("ug1", [P, 2, 2, H * T])
        exp1 = sb("exp1", [P, 2, H * T])
        exp2 = sb("exp2", [P, 2, T])
        E1 = sb("E1", [P, T, H])
        E2 = sb("E2", [P, T])
        grow1 = sb("grow1", [H * T, P])
        G1 = sb("G1", [P, 2, N])
        amax2 = sb("amax2", [P, 1])
        A2 = sb("A2", [P, 1])
        aC2 = sb("aC2", [P, T])
        bC2 = sb("bC2", [P, T])
        ug2 = sb("ug2", [P, 2, T])
        grow2 = grow1[0:T, :]
        G2 = sb("G2", [P, N])
        den = sb("den", [P, 4])
        rden = sb("rden", [P, 4])
        z0 = sb("z0", [P, 4, P])
        z = sb("z", [P, GB * P])
        e = sb("e", [P, GB * P])
        y = sb("y", [P, XR, D])
        rden2 = sb("rden2", [P, 4])
        squares = sb("squares", [P, D], F16)
        norms = sb("norms", [P, 3, T])
        extremes = sb("extremes", [P, 2, 2])
        bounds = sb("bounds", [P, 3, 2])
        bounds_all = sb("bounds_all", [P, 3, 2])
        within = sb("within", [P, 6])
        verdict = sb("verdict", [P, 1], I32)
        stats = sb("stats", [P, 4, 6])
        mv = sb("mv", [P, 4, 2])
        rstd = sb("rstd", [P, 4, 2])

        def one_pass(split, pass_ctx, semaphores):
            def sem(name):
                semaphores.append(nc.alloc_semaphore(f"{name}_{'split' if split else 'general'}"))
                return semaphores[-1]

            params1_loaded = sem("params1_loaded")
            params2_loaded = sem("params2_loaded")
            ident_cleared = sem("ident_cleared")
            ident_ready = sem("ident_ready")
            const_ready = sem("const_ready")
            fold_product = sem("fold_product")
            fold2_product = sem("fold2_product")
            w1_ready = sem("w1_ready")
            w2_ready = sem("w2_ready")
            adj_loaded = [sem(f"adj_loaded{k}") for k in range(2)]
            x_loaded = [sem(f"x_loaded{k}") for k in range(XR)]
            res_loaded = [sem(f"res_loaded{k}") for k in range(XR)]
            out_stored = [sem(f"out_stored{k}") for k in range(XR)]
            mask_compared = sem("mask_compared")
            mask_ready = sem("mask_ready")
            p1_ready = sem("p1_ready")
            p2_ready = sem("p2_ready")
            agg1_done = sem("agg1_done")
            agg2_done = sem("agg2_done")
            den_copied = sem("den_copied")
            rden_ready = sem("rden_ready")
            z0_ready = sem("z0_ready")
            z_ready = sem("z_ready")
            t_ready = sem("t_ready")
            e_ready = sem("e_ready")
            htr_done = sem("htr_done")
            hT_ready = sem("hT_ready")
            xtr_done = sem("xtr_done")
            xT_ready = sem("xT_ready")
            proj1_done = sem("proj1_done")
            v1_raw = sem("v1_raw")
            norms1_ready = sem("norms1_ready")
            xT_high = sem("xT_high")
            w1_high = sem("w1_high")
            w1_parted = sem("w1_parted")
            proj2_done = sem("proj2_done")
            v2_raw = sem("v2_raw")
            amax_ready = sem("amax_ready")
            A1_ready = sem("A1_ready")
            shifted1 = sem("shifted1")
            clamped1 = sem("clamped1")
            E1_ready = sem("E1_ready")
            exp1_ready = sem("exp1_ready")
            hi1_packed = sem("hi1_packed")
            ug1_ready = sem("ug1_ready")
            grow1_turned = sem("grow1_turned")
            grow1_ready = sem("grow1_ready")
            g1_stored = sem("g1_stored")
            G1_loaded = [sem(f"G1_loaded{q}") for q in range(2)]
            mask_copied = sem("mask_copied")
            v1_hi = sem("v1_hi")
            v1_lo = sem("v1_lo")
            bounds1_taken = sem("bounds1_taken")
            bounds2_taken = sem("bounds2_taken")
            bounds_ready = sem("bounds_ready")
            bounds_reduced = sem("bounds_reduced")
            compared = sem("compared")
            amax2_ready = sem("amax2_ready")
            A2_ready = sem("A2_ready")
            shifted2 = sem("shifted2")
            clamped2 = sem("clamped2")
            E2_ready = sem("E2_ready")
            exp2_ready = sem("exp2_ready")
            hi2_packed = sem("hi2_packed")
            ug2_ready = sem("ug2_ready")
            grow2_turned = sem("grow2_turned")
            grow2_ready = sem("grow2_ready")
            g2_stored = sem("g2_stored")
            G2_loaded = sem("G2_loaded")
            v2_hi = sem("v2_hi")
            v2_lo = sem("v2_lo")
            v1_ready, v2_ready = (v1_lo, v2_lo) if split else (v1_hi, v2_hi)
            res_biased = sem("res_biased")
            rden2_ready = sem("rden2_ready")
            y_summed = sem("y_summed")
            stats_ready = sem("stats_ready")
            mv_ready = sem("mv_ready")
            var_ready = sem("var_ready")
            rstd_ready = sem("rstd_ready")
            y_ready = sem("y_ready")

            held = sem("held")

            def hold(engine, semaphore, value):
                engine.wait_ge(semaphore, value)
                engine.sem_inc(held, 1)

            reach = SPLIT_RANGE if split else RANGE

            def has(i):
                if isinstance(i, int):
                    return 0 <= i < B, i >= 1, i < B - 1
                return True, True, True

            def first(i, n):
                return isinstance(i, int) and i < n

            def proj1_slot(i, n):
                return (n + 2, n) if first(i, 0) else (L_PROJ1[n], L_PROJ1[n] - 2)

            def mask_slot(i, s):
                return s + 1 if first(i, 0) else L_PROJ1[s]

            def proj1_banks(i, n):
                return acc[2 * (n % 2):2 * (n % 2) + 2] if first(i, 0) else (proj_ps, misc_ps)

            def v1_slot(i, n):
                return L_GROW1 + 2 if first(i, 0) else S1 + n

            def blocks1(i, u, d):
                together = first(i, 1) and u == 0 and d < 4
                return (range(4) if d == 0 else ()) if together else (d,)

            def blocks2(i, d):
                together = not has(i)[0] and d < 4
                return (range(4) if d == 0 else ()) if together else (d,)

            def run(engine, body):
                body(-1, 1)
                body(0, 0)
                with engine.Fori(1, B - 2, 2) as i:
                    body(i, 1)
                    body(i + 1, 0)
                body(B - 1, 1)
                body(B, 0)

            def when_needed(engine, program):
                if split:
                    program()
                else:
                    in_bounds = engine.value_load(verdict[0:1, 0:1], min_val=0, max_val=1)
                    with engine.If(in_bounds == 0):
                        program()

            block = pass_ctx.enter_context(nc.Block())

            @block.sync
            def _(sp):
                def load_x(b, n, i):
                    if not first(i, 0) or n >= XR:
                        hold(sp, xtr_done, b * T + n - XR + 1)
                    sp.dma_start(x_t[:, n % XR, :], x[b, n * P:(n + 1) * P, :]).then_inc(x_loaded[n % XR], 16)

                def load_adj(b, s, i):
                    if not first(i, 0) or s >= 2:
                        hold(sp, mask_compared, b * T + s - 1)
                    sp.dma_start(adj_t[s % 2][:], adj[b, s * P:(s + 1) * P, :]).then_inc(adj_loaded[s % 2], 16)

                def load_G1(b, q):
                    sp.dma_start(G1[:, q % 2, :], g1_rows[q].partition_broadcast(P)).then_inc(G1_loaded[q % 2], 16)

                def load_residual(b, d, i):
                    hold(sp, out_stored[d % XR], 16 * (2 * b + d // XR + 1))
                    sp.dma_start(y[:, d % XR, :], x[b, d * P:(d + 1) * P, :]).then_inc(res_loaded[d % XR], 16)

                def store_y(b, d):
                    hold(sp, y_ready, b * T + d + 1)
                    sp.dma_start(out[b, d * P:(d + 1) * P, :], y[:, d % XR, :]).then_inc(out_stored[d % XR], 16)

                def body(i, par):
                    l1, l2, nxt = has(i)
                    for L in range(SLOTS + 2):
                        if l1 and L in (0, T):
                            q = 2 + L // T
                            hold(sp, p1_ready, i * S1 + (q - 1) * T)
                            load_G1(i, q)
                        if l1 and L == S1:
                            hold(sp, p1_ready, S1 * (i + 1))
                            if l2:
                                hold(sp, p2_ready, i * T)
                            sp.dma_start(mask2[:], mask[:, par, :, :]).then_inc(mask_copied, 16)
                        if nxt and L == 0 and not first(i, 0):
                            for s in range(2):
                                load_adj(i + 1, s, i)
                            for n in range(XR):
                                load_x(i + 1, n, i)
                        for n in range(XR, T):
                            if nxt and L == proj1_slot(i, n - XR)[1] + 1:
                                load_x(i + 1, n, i)
                        if l2 and L == L_GROW2 + 2:
                            hold(sp, grow2_ready, i)
                            sp.dma_start(g2_rows.rearrange("a (t c) -> (a t) c", c=P), grow2).then_inc(g2_stored, 16)
                            hold(sp, g2_stored, 16 * i)
                            sp.dma_start(G2[:], g2_rows[0].partition_broadcast(P)).then_inc(G2_loaded, 16)
                        if nxt and L == L_GROW1 + 1:
                            if l1:
                                hold(sp, p1_ready, S1 * (i + 1))
                            hold(sp, grow1_ready, i + 2)
                            sp.dma_start(g1_rows.rearrange("h (t c) -> (h t) c", c=P), grow1[:]).then_inc(g1_stored, 16)
                            hold(sp, g1_stored, 16 * (i + 2))
                            for q in range(2):
                                load_G1(i + 1, q)
                        if l2 and L in range(L_P2 + 3, L_P2 + 3 + XR):
                            load_residual(i - 1, L - L_P2 - 3, i)
                        for s in range(2, T):
                            if nxt and L == mask_slot(i, s - 2):
                                load_adj(i + 1, s, i)
                        d = L - S1 - 2
                        if l2 and 0 <= d < T:
                            store_y(i - 1, d)
                            if d >= 1 and d - 1 + XR < T:
                                load_residual(i - 1, d - 1 + XR, i)

                def start():
                    sp.sem_inc(y_summed, T)
                    sp.sem_inc(agg2_done, T)
                    for k in range(XR):
                        sp.sem_inc(out_stored[k], 16)
                    for n in range(XR):
                        load_x(0, n, -1)
                    if split:
                        for dst, src in (
                            (w1_whole[:, :, 0:HF // 2], W1.rearrange("(c p) n -> p c n", p=P)[:, :, 0:HF // 2]),
                            (w1_whole[:, :, WA:], W1.rearrange("(c p) n -> p c n", p=P)[:, :, HF // 2:]),
                            (p[:, 0, 0, 0:HF], att_src1.rearrange("h f -> (h f)").partition_broadcast(P)),
                            (p[:, 0, 0, HF:2 * HF], att_dst1.rearrange("h f -> (h f)").partition_broadcast(P)),
                        ):
                            sp.dma_start(dst, src).then_inc(params1_loaded, 16)
                    for s in range(2):
                        load_adj(0, s, -1)
                    if split:
                        for dst, src in (
                            (w2[:, :, 0:D], W2.rearrange("(c p) n -> p c n", p=P)),
                            (att2[:, 0:D], att_src2.rearrange("h f -> (h f)").partition_broadcast(P)),
                            (att2[:, D:2 * D], att_dst2.rearrange("h f -> (h f)").partition_broadcast(P)),
                            (bias2[:], b2.partition_broadcast(P)),
                        ):
                            sp.dma_start(dst, src).then_inc(params2_loaded, 16)
                        sp.dma_start(bias1[:], b1.rearrange("(h f) -> f h", f=F),
                                     allow_slow_non_contiguous=True).then_inc(params2_loaded, 16)

                def program():
                    start()
                    run(sp, body)
                    for k in range(XR):
                        sp.wait_ge(out_stored[k], 16 * (B * T // XR + 1))

                when_needed(sp, program)

            @block.tensor
            def _(pe):
                def transpose_x(b, n, i):
                    pe.wait_ge(x_loaded[n % XR], 16 * (2 * b + n // XR + 1))
                    if not first(i, 0) or n >= 1:
                        pe.wait_ge(xT_ready, b * T + n)
                    for c in range(KC):
                        last = nc.tensor.transpose(xtr_ps[:, c * P:(c + 1) * P], x_t[:, n % XR, c * P:(c + 1) * P], ident[:])
                    last.then_inc(xtr_done, 1)

                def project1(b, n, i):
                    pe.wait_ge(xT_ready, b * T + n + 1)
                    dst_a, dst_b = proj1_banks(i, n)
                    if first(i, 0):
                        if n == 0 and split:
                            pe.wait_ge(w1_ready, 1)
                        if n >= 2:
                            pe.wait_ge(v1_raw, b * T + n - 1)
                    elif n == 0:
                        if not first(i, 1):
                            pe.wait_ge(v2_raw, i * T)
                        pe.wait_ge(grow1_ready, i + 1)
                        if has(i)[1]:
                            pe.wait_ge(grow2_ready, i)
                    else:
                        pe.wait_ge(v1_raw, b * T + n)
                    for dst, cols in ((dst_a[:, 0:WA], slice(0, WA)), (dst_b[:, 0:HF // 2], slice(WA, HF + NA))):
                        steps = [(x_part, w_part, c) for x_part, w_part in ((0, 1), (0, 0), (1, 0)) for c in range(KC)]
                        for k, (x_part, w_part, c) in enumerate(steps):
                            last = nc.tensor.matmul(dst, xT[:, n % 2, x_part, c, :],
                                                    w1[:, w_part, c, cols],
                                                    start=(k == 0), stop=(k == len(steps) - 1))
                    last.then_inc(proj1_done, 1)

                def transpose_h(i, m):
                    pe.wait_ge(z0_ready, i * S1 + m + 1)
                    if m % GB == 0 and (not first(i, 1) or m >= 1):
                        pe.wait_ge(z_ready, i * GROUPS + m // GB)
                    nc.tensor.transpose(htr_ps[:, (m % GB) * P:(m % GB + 1) * P], z0[:, m % 4, :], ident[:]).then_inc(htr_done, 1)

                def project2(i, n):
                    if split and n == 0 and first(i, 1):
                        pe.wait_ge(w2_ready, 1)
                    if n % GB == 0:
                        pe.wait_ge(hT_ready, i * GROUPS + ((H - 1) * T + n) // GB + 1)
                    if n >= 1:
                        pe.wait_ge(v2_raw, i * T + n)
                    elif has(i)[2]:
                        pe.wait_ge(v1_raw, (i + 2) * T)
                    else:
                        pe.wait_ge(v2_raw, i * T)
                    for c in range(FC):
                        last = nc.tensor.matmul(proj_ps[:, 0:V2W], hT[:, c, n * P:(n + 1) * P], w2[:, c, :],
                                                start=(c == 0), stop=(c == FC - 1))
                    last.then_inc(proj2_done, 1)

                def products(dst, buf, s, d, v, v_hi, v_lo):
                    block = slice(d * P, (d + 1) * P)
                    if not split:
                        return nc.tensor.matmul(dst, p[:, buf, s, block], v, start=(s == 0), stop=(s == T - 1))
                    p_hi, p_lo = p_pair[:, buf, s, block, 1], p_pair[:, buf, s, block, 0]
                    nc.tensor.matmul(dst, p_hi, v_lo, start=(s == 0), stop=False)
                    nc.tensor.matmul(dst, p_hi, v_hi, start=False, stop=False)
                    return nc.tensor.matmul(dst, p_lo, v_hi, start=False, stop=(s == T - 1))

                def aggregate1(i, par, u, blocks):
                    for d in blocks:
                        m = u * T + d
                        if m >= 4:
                            pe.wait_ge(z0_ready, i * S1 + m - 3)
                        elif not first(i, 1):
                            pe.wait_ge(y_summed, i * T + m - 3)
                    for s in range(T):
                        if 0 in blocks:
                            if u == 0:
                                pe.wait_ge(v1_ready, i * T + s + 1)
                            pe.wait_ge(p1_ready, i * S1 + u * T + s + 1)
                        for d in blocks:
                            last = products(acc[d % 4][:, 0:F + 1], (par + u) % 2, s, d, v1[:, s, u, 0:F + 1],
                                            v1s[:, s, u, 0, 0:F + 1], v1s[:, s, u, 1, 0:F + 1])
                            if s == T - 1:
                                last.then_inc(agg1_done, 1)

                def aggregate2(i, par, blocks):
                    for d in blocks:
                        if d >= 4:
                            pe.wait_ge(y_summed, i * T + d - 3)
                        elif has(i)[0]:
                            pe.wait_ge(z0_ready, i * S1 + S1 + d - 3)
                        else:
                            pe.wait_ge(y_summed, i * T + d - 3)
                    for s in range(T):
                        if 0 in blocks:
                            pe.wait_ge(v2_ready, (i - 1) * T + s + 1)
                            pe.wait_ge(p2_ready, (i - 1) * T + s + 1)
                        for d in blocks:
                            last = products(acc[d % 4][:, 0:D + 1], par, s, d, v2[:, s, 0:D + 1],
                                            v2s[:, s, 0, 0:D + 1], v2s[:, s, 1, 0:D + 1])
                            if s == T - 1:
                                last.then_inc(agg2_done, 1)

                def body(i, par):
                    l1, l2, nxt = has(i)
                    for L in range(SLOTS):
                        if l1 and L < S1:
                            aggregate1(i, par, L // T, blocks1(i, L // T, L % T))
                        if l2 and L >= S1:
                            aggregate2(i, par, blocks2(i, L - S1))
                        if l2 and L == L_GROW2:
                            pe.wait_ge(ug2_ready, i)
                            if l1:
                                pe.wait_ge(grow1_ready, i + 1)
                            nc.tensor.transpose(misc_ps[0:T, 2 * P:3 * P], ug2[:, 1, :], ident[:]).then_inc(grow2_turned, 1)
                        for n in range(T):
                            if nxt and L == proj1_slot(i, n)[0]:
                                project1(i + 1, n, i)
                        for n in range(T):
                            if nxt and L == proj1_slot(i, n)[1]:
                                transpose_x(i + 1, n, i)
                        if nxt and L == L_GROW1:
                            pe.wait_ge(ug1_ready, i + 2)
                            pe.wait_ge(v1_raw, (i + 2) * T)
                            nc.tensor.transpose(misc_ps[0:H * T, 2 * P:3 * P], ug1[:, 1 - par, 1, :],
                                                ident[:]).then_inc(grow1_turned, 1)
                        for m in range(S1):
                            if l1 and L == htr_slot[m]:
                                transpose_h(i, m)
                        if l1 and L >= S1:
                            project2(i, L - S1)

                def program():
                    if split:
                        pe.wait_ge(ident_ready, 1)
                    run(pe, body)

                when_needed(pe, program)

            @block.scalar
            def _(act):
                def copy_den1(i, m):
                    act.wait_ge(agg1_done, i * S1 + m + 1)
                    nc.scalar.copy(den[:, m % 4:m % 4 + 1], acc[m % 4][:, F:F + 1]).then_inc(den_copied, 1)

                def normalise1(i, m):
                    act.wait_ge(rden_ready, i * S1 + m + 1)
                    if not first(i, 1) or m >= 4:
                        act.wait_ge(htr_done, i * S1 + m - 3)
                    nc.scalar.activation(z0[:, m % 4, :], acc[m % 4][:, 0:F], ACT.Copy,
                                         scale=rden[:, m % 4:m % 4 + 1]).then_inc(z0_ready, 1)

                def elu_exp(i, g):
                    q = g * GB // T
                    act.wait_ge(htr_done, i * S1 + (g + 1) * GB)
                    if not first(i, 1) or g >= 1:
                        act.wait_ge(hT_ready, i * GROUPS + g)
                    elif split:
                        act.wait_ge(params2_loaded, 16 * 5)
                    nc.scalar.activation(z[:], htr_ps[:], ACT.Identity, bias=bias1[:, q:q + 1]).then_inc(z_ready, 1)
                    act.wait_ge(z_ready, i * GROUPS + g + 1)
                    nc.scalar.activation(e[:], z[:], ACT.Relu, scale=-1.0).then_inc(t_ready, 1)
                    act.wait_ge(t_ready, i * GROUPS + g + 1)
                    nc.scalar.activation(e[:], e[:], ACT.Exp, scale=-1.0).then_inc(e_ready, 1)

                def high_part_xT(b, n, i):
                    act.wait_ge(xtr_done, b * T + n + 1)
                    if not first(i, 0) or n >= 2:
                        act.wait_ge(proj1_done, b * T + n - 1)
                    nc.scalar.copy(xT[:, n % 2, 0, :, :].rearrange("p c n -> p (c n)"), xtr_ps[:, 0:KC * P]).then_inc(xT_high, 1)

                def copy_raw1(b, n, i):
                    act.wait_ge(proj1_done, b * T + n + 1)
                    src_a, src_b = proj1_banks(i, n)
                    if n == 0 and not first(i, 0):
                        act.wait_ge(v1_ready, b * T)
                    nc.scalar.mul(raw1[:, n, 0:HF // 2], src_a[:, 0:HF // 2], VSCALE)
                    nc.scalar.copy(ab[:, n, :], src_a[:, HF // 2:WA])
                    nc.scalar.mul(raw1[:, n, HF // 2:HF], src_b[:, 0:HF // 2], VSCALE).then_inc(v1_raw, 1)

                def take_norms1(b, n, i):
                    if split:
                        act.wait_ge(v1_raw, b * T + n + 1)
                        for k in range(2):
                            if k == 1 or not first(i, 0) or n >= 1:
                                act.wait_ge(norms1_ready, 2 * (b * T + n) + k)
                            nc.scalar.activation(squares[:], raw1[:, n, k * D:(k + 1) * D], ACT.Square, scale=1.0 / VSCALE,
                                                 accum_out=norms[:, k, n:n + 1]).then_inc(norms1_ready, 1)

                def finish_v1(b, n, l1):
                    if n == 0:
                        act.wait_ge(E1_ready, b + 1)
                        act.wait_ge(v1_raw, (b + 1) * T)
                        if l1:
                            act.wait_ge(agg1_done, b * S1)
                        nc.scalar.mul(v1s[:, :, :, 0, F] if split else v1[:, :, :, F], E1[:], VSCALE)
                    dst = v1s[:, n, :, 0, 0:F] if split else v1[:, n, :, 0:F]
                    for q in range(H):
                        last = nc.scalar.activation(dst[:, q, :], raw1[:, n, q * F:(q + 1) * F], ACT.Copy, scale=E1[:, n, q:q + 1])
                    last.then_inc(v1_hi, 1)

                def finish_v2(i, n):
                    if n == 0:
                        act.wait_ge(E2_ready, i)
                        act.wait_ge(v2_raw, i * T)
                        act.wait_ge(agg2_done, i * T)
                        nc.scalar.mul(v2s[:, :, 0, D] if split else v2[:, :, D], E2[:], VSCALE)
                    dst = v2s[:, n, 0, 0:D] if split else v2[:, n, 0:D]
                    nc.scalar.activation(dst, raw2[:, n, 0:D], ACT.Copy, scale=E2[:, n:n + 1]).then_inc(v2_hi, 1)

                def copy_raw2(i, n):
                    act.wait_ge(proj2_done, i * T + n + 1)
                    if n == 0 and not first(i, 1):
                        act.wait_ge(v2_ready, i * T)
                    if split:
                        nc.scalar.activation(squares[:, 0:D], proj_ps[:, 0:D], ACT.Square, accum_out=norms[:, 2, n:n + 1])
                    nc.scalar.mul(raw2[:, n, :], proj_ps[:, 0:V2W], VSCALE).then_inc(v2_raw, 1)

                def body(i, par):
                    l1, l2, nxt = has(i)
                    for L in range(SLOTS + 1):
                        if l1 and 1 <= L <= S1:
                            copy_den1(i, L - 1)
                        for n in range(T):
                            if nxt and L == proj1_slot(i, n)[1] + 1:
                                high_part_xT(i + 1, n, i)
                        for n in range(T):
                            if nxt and L == proj1_slot(i, n)[0] + 1:
                                copy_raw1(i + 1, n, i)
                        if l1 and S1 < L <= SLOTS:
                            copy_raw2(i, L - S1 - 1)
                        if l1 and 2 <= L <= S1 + 1:
                            normalise1(i, L - 2)
                        if l2 and L == L_CHAIN2 + 4:
                            act.wait_ge(clamped2, i)
                            nc.scalar.activation(E2[:], aC2[:], ACT.Exp).then_inc(E2_ready, 1)
                            nc.scalar.activation(exp2[:, 1, :], bC2[:], ACT.Exp, scale=GAP).then_inc(exp2_ready, 1)
                            nc.scalar.activation(exp2[:, 0, :], aC2[:], ACT.Exp, scale=-GAP).then_inc(exp2_ready, 1)
                        if l2 and L == L_GROW2 + 1:
                            act.wait_ge(grow2_turned, i)
                            act.wait_ge(g1_stored, 16 * (i + 1) if l1 else 16 * B)
                            nc.scalar.copy(grow2, misc_ps[0:T, 2 * P:3 * P]).then_inc(grow2_ready, 1)
                        if nxt and L == L_CHAIN1 + 4:
                            act.wait_ge(clamped1, 2 * (i + 2))
                            nc.scalar.activation(E1[:], aC[:], ACT.Exp).then_inc(E1_ready, 1)
                            nc.scalar.activation(exp1[:, 1, :].rearrange("p (h t) -> p h t", h=H),
                                                 bC[:].rearrange("p t h -> p h t"), ACT.Exp, scale=GAP).then_inc(exp1_ready, 1)
                            nc.scalar.activation(exp1[:, 0, :].rearrange("p (t h) -> p t h", h=H),
                                                 aC[:], ACT.Exp, scale=-GAP).then_inc(exp1_ready, 1)
                        if nxt and L == L_GROW1 + 1:
                            act.wait_ge(grow1_turned, i + 2)
                            if not first(i, 0):
                                act.wait_ge(g1_stored, 16 * (i + 1))
                            if l2:
                                act.wait_ge(g2_stored, 16 * i)
                            nc.scalar.copy(grow1[:], misc_ps[0:H * T, 2 * P:3 * P]).then_inc(grow1_ready, 1)
                        if l1 and L in elu_slot:
                            elu_exp(i, elu_slot.index(L))
                        for n in range(T):
                            if nxt and L == proj1_slot(i, n)[0] + 1:
                                take_norms1(i + 1, n, i)
                        if l2 and 0 <= L - L_HIGH2 < T:
                            finish_v2(i, L - L_HIGH2)
                        for n in range(T):
                            if nxt and L == v1_slot(i, n):
                                finish_v1(i + 1, n, l1)

                def program():
                    run(act, body)

                when_needed(act, program)

            @block.gpsimd
            def _(pool):
                def invert1(i, m):
                    pool.wait_ge(den_copied, i * S1 + m + 1)
                    nc.gpsimd.tensor_tensor(rden[:, m % 4:m % 4 + 1], den[:, m % 4:m % 4 + 1], minus_one[:],
                                            ALU.pow).then_inc(rden_ready, 1)

                def inverse_deviation(b, d):
                    pool.wait_ge(var_ready, b * T + d + 1)
                    nc.gpsimd.tensor_tensor(rstd[:, d % 4, 1:2], rstd[:, d % 4, 0:1], halfpow[:], ALU.pow).then_inc(rstd_ready, 1)

                def add_own_edges(b, par, s):
                    hold(pool, mask_compared, b * T + s + 1)
                    own = mask[:, par, s, s * P:(s + 1) * P].bitcast(mybir.dt.int8)
                    nc.gpsimd.affine_select(out=own, in_=own, compare_op=ALU.not_equal, fill=1.0, base=0,
                                            pattern=[[-1, P]], channel_multiplier=1).then_inc(mask_ready, 1)

                def bias_residual(b, d):
                    pool.wait_ge(res_loaded[d % XR], 16 * (2 * b + d // XR + 1))
                    nc.gpsimd.tensor_tensor(y[:, d % XR, :], y[:, d % XR, :], bias2[:], ALU.add).then_inc(res_biased, 1)

                def body(i, par):
                    l1, l2, nxt = has(i)
                    for L in range(SLOTS + 1):
                        if l1 and 1 <= L <= S1:
                            invert1(i, L - 1)
                        for n in range(T):
                            if nxt and L == mask_slot(i, n):
                                add_own_edges(i + 1, 1 - par, n)
                        if l2 and L == L_CHAIN2 + 1:
                            hold(pool, amax2_ready, i)
                            nc.gpsimd.partition_all_reduce(A2[:], amax2[:], P, RMAX).then_inc(A2_ready, 1)
                        if split and not l1 and l2 and L == L_JUDGE:
                            pool.wait_ge(bounds_ready, 1)
                            nc.gpsimd.partition_all_reduce(bounds_all[:].rearrange("p k l -> p (k l)"),
                                                           bounds[:].rearrange("p k l -> p (k l)"), P, RMAX).then_inc(bounds_reduced, 1)
                        if nxt and L == L_CHAIN1 + 2:
                            hold(pool, amax_ready, i + 2)
                            nc.gpsimd.partition_all_reduce(A1[:], amax[:], P, RMAX).then_inc(A1_ready, 1)
                        if l2 and 1 <= L - S1 <= T:
                            inverse_deviation(i - 1, L - S1 - 1)
                        if l2 and 0 <= L - (S1 - 1) < T:
                            bias_residual(i - 1, L - (S1 - 1))

                def start():
                    nc.gpsimd.memset(halfpow[:], -0.5).then_inc(const_ready, 1)
                    nc.gpsimd.memset(minus_one[:], -1.0).then_inc(const_ready, 1)
                    nc.gpsimd.memset(ident[:], 0.0).then_inc(ident_cleared, 1)
                    pool.wait_ge(ident_cleared, 1)
                    nc.gpsimd.affine_select(out=ident[:], in_=ident[:], compare_op=ALU.not_equal, fill=1.0, base=0,
                                            pattern=[[-1, P]], channel_multiplier=1).then_inc(ident_ready, 1)
                    pool.wait_ge(const_ready, 2)
                    pool.wait_ge(params2_loaded, 16 * 5)

                def program():
                    if split:
                        start()
                    run(pool, body)

                when_needed(pool, program)

            @block.vector
            def _(dve):
                def make_mask(b, par, s):
                    if s == 0 and not first(b, 2):
                        dve.wait_ge(mask_copied, 16 * (b - 1))
                    dve.wait_ge(adj_loaded[s % 2], 16 * (4 * b + s // 2 + 1))
                    nc.vector.tensor_scalar(mask[:, par, s, :], adj_t[s % 2][:], 0.0, None, ALU.is_gt).then_inc(mask_compared, 1)

                def weights1(b, par, u, s):
                    if u == 0:
                        dve.wait_ge(mask_ready, b * T + s + 1)
                    if s == 0:
                        dve.wait_ge(G1_loaded[u % 2], 16 * (2 * b + u // 2 + 1))
                    nc.vector.scalar_tensor_tensor(out=p[:, (par + u) % 2, s, :], in0=G1[:, u % 2, :], scalar=ug1[:, par, 0, s * H + u:s * H + u + 1],
                                                   in1=mask[:, par, s, :], op0=ALU.max, op1=ALU.mult).then_inc(p1_ready, 1)

                def weights2(i, par, s):
                    if s == 0:
                        dve.wait_ge(G2_loaded, 16 * i)
                        dve.wait_ge(mask_copied, 16 * i)
                    nc.vector.scalar_tensor_tensor(out=p[:, par, s, :], in0=G2[:], scalar=ug2[:, 0, s:s + 1],
                                                   in1=mask2[:, s, :], op0=ALU.max, op1=ALU.mult).then_inc(p2_ready, 1)

                def elu(i, g):
                    q, part = g * GB // T, g % (T // GB)
                    dve.wait_ge(e_ready, i * GROUPS + g + 1)
                    if g == 0 and not first(i, 1):
                        dve.wait_ge(proj2_done, i * T)
                    nc.vector.scalar_tensor_tensor(out=hT[:, q, part * GB * P:(part + 1) * GB * P], in0=e[:], scalar=-1.0,
                                                   in1=z[:], op0=ALU.add, op1=ALU.max).then_inc(hT_ready, 1)

                def invert2(i, d):
                    q = (i - 1) * T + d + 1
                    dve.wait_ge(agg2_done, i * T + d + 1)
                    nc.vector.reciprocal(rden2[:, d % 4:d % 4 + 1], acc[d % 4][:, D:D + 1]).then_inc(rden2_ready, 1)

                def residual(i, d):
                    q = (i - 1) * T + d + 1
                    dve.wait_ge(rden2_ready, q)
                    dve.wait_ge(res_biased, q)
                    nc.vector.scalar_tensor_tensor(out=y[:, d % XR, :], in0=acc[d % 4][:, 0:D], scalar=rden2[:, d % 4:d % 4 + 1],
                                                   in1=y[:, d % XR, :], op0=ALU.mult, op1=ALU.add).then_inc(y_summed, 1)

                def moments(i, d):
                    q = (i - 1) * T + d + 1
                    dve.wait_ge(y_summed, q + T)
                    nc.vector.bn_stats(stats[:, d % 4, :], y[:, d % XR, :]).then_inc(stats_ready, 1)
                    hold(dve, stats_ready, q)
                    nc.vector.bn_aggr(mv[:, d % 4, :], stats[:, d % 4, :]).then_inc(mv_ready, 1)
                    dve.wait_ge(mv_ready, q)
                    nc.vector.tensor_scalar(rstd[:, d % 4, 0:1], mv[:, d % 4, 1:2], EPS, None, ALU.add).then_inc(var_ready, 1)

                def layer_norm(i, d):
                    dve.wait_ge(rstd_ready, (i - 1) * T + d + 1)
                    nc.vector.tensor_scalar(y[:, d % XR, :], y[:, d % XR, :], mv[:, d % 4, 0:1], rstd[:, d % 4, 1:2],
                                            ALU.subtract, ALU.mult).then_inc(y_ready, 1)

                def take_bounds(taken, made, n, layer, a_least):
                    dve.wait_ge(taken, n * 5 + made)
                    of_layer = norms[:, 0:2, :] if layer == 0 else norms[:, 2:3, :]
                    of_layer = of_layer.rearrange("p k t -> p (k t)")
                    nc.vector.tensor_reduce(extremes[:, layer, 0:1], of_layer, AX.X, ALU.max).then_inc(taken, 1)
                    nc.vector.tensor_reduce(extremes[:, layer, 1:2], a_least, AX.X, ALU.min).then_inc(taken, 1)
                    dve.wait_ge(taken, n * 5 + made + 2)
                    for k, e_k, op in ((0, 0, ALU.max), (1, 0, ALU.min), (2, 1, ALU.min)):
                        bound = bounds[:, k, layer:layer + 1]
                        nc.vector.tensor_tensor(bound, bound, extremes[:, layer, e_k:e_k + 1], op).then_inc(taken, 1)

                def pack(word, value, hi_packed, ready, k):
                    if not split:
                        nc.vector.tensor_copy(word, value).then_inc(ready, 1)
                        return
                    pair = word.bitcast(F16).rearrange("p (n k) -> p n k", k=2)
                    nc.vector.tensor_scalar(pair[:, :, 1], value, HI_FACTOR, None, ALU.mult).then_inc(hi_packed, 1)
                    dve.wait_ge(hi_packed, k)
                    nc.vector.tensor_tensor(pair[:, :, 0], value, pair[:, :, 1], ALU.subtract).then_inc(ready, 1)

                def low_part_xT(b, n, i):
                    dve.wait_ge(xT_high, b * T + n + 1)
                    high, low = (xT[:, n % 2, k, :, :].rearrange("p c n -> p (c n)") for k in range(2))
                    nc.vector.tensor_tensor(low, xtr_ps[:, 0:KC * P], high, ALU.subtract).then_inc(xT_ready, 1)

                def factors1(i, par, L):
                    k = i + 2
                    a, b = ab[:, :, 0:H], ab[:, :, H:NA]
                    if L == 0:
                        dve.wait_ge(v1_raw, k * T)
                        nc.vector.tensor_reduce(amax[:], a.rearrange("p t h -> p h t"), AX.X, ALU.max).then_inc(amax_ready, 1)
                    if L == 3:
                        dve.wait_ge(A1_ready, k)
                        A = A1[:].unsqueeze(1).broadcast_to([P, T, H])
                        nc.vector.tensor_tensor(bC[:], b, A, ALU.add).then_inc(shifted1, 1)
                        nc.vector.tensor_tensor(aC[:], a, A, ALU.subtract).then_inc(shifted1, 1)
                        dve.wait_ge(shifted1, 2 * k)
                        if split:
                            dve.wait_ge(norms1_ready, 2 * k * T)
                            take_bounds(bounds1_taken, 1, i + 1, 0, aC[:].rearrange("p t h -> p (t h)"))
                            dve.wait_ge(bounds1_taken, 5 * k + 1)
                        nc.vector.tensor_scalar(bC[:], bC[:], reach, G_FLOOR, ALU.min, ALU.max).then_inc(clamped1, 1)
                        nc.vector.tensor_scalar(aC[:], aC[:], -reach, None, ALU.max).then_inc(clamped1, 1)
                    if L == 5:
                        dve.wait_ge(exp1_ready, 2 * k)
                        pack(ug1[:, 1 - par, :, :].rearrange("p k n -> p (k n)"), exp1[:].rearrange("p k n -> p (k n)"),
                             hi1_packed, ug1_ready, k)

                def factors2(i, par, L):
                    a, b = raw2[:, :, D], raw2[:, :, D + 1]
                    if L == 0:
                        dve.wait_ge(v2_raw, i * T)
                        nc.vector.tensor_reduce(amax2[:], a, AX.X, ALU.max).then_inc(amax2_ready, 1)
                    if L == 3:
                        dve.wait_ge(A2_ready, i)
                        nc.vector.tensor_scalar(bC2[:], b, A2[:, 0:1], reach, ALU.add, ALU.min).then_inc(shifted2, 1)
                        nc.vector.tensor_scalar(aC2[:], a, A2[:, 0:1], -reach, ALU.subtract, ALU.max).then_inc(shifted2, 1)
                        dve.wait_ge(shifted2, 2 * i)
                        if split:
                            take_bounds(bounds2_taken, 2, i - 1, 1, aC2[:])
                        nc.vector.tensor_scalar(bC2[:], bC2[:], G_FLOOR, None, ALU.max).then_inc(clamped2, 1)
                    if L == 5:
                        dve.wait_ge(exp2_ready, 2 * i)
                        pack(ug2[:].rearrange("p k n -> p (k n)"), exp2[:].rearrange("p k n -> p (k n)"),
                             hi2_packed, ug2_ready, i)

                def low_part1(n, b):
                    dve.wait_ge(v1_hi, b * T + n + 1)
                    if n == 0:
                        nc.vector.scalar_tensor_tensor(out=v1s[:, :, :, 1, F], in0=E1[:], scalar=VSCALE,
                                                       in1=v1s[:, :, :, 0, F], op0=ALU.mult, op1=ALU.subtract)
                    for q in range(H):
                        last = nc.vector.scalar_tensor_tensor(out=v1s[:, n, q, 1, 0:F], in0=raw1[:, n, q * F:(q + 1) * F],
                                                              scalar=E1[:, n, q:q + 1], in1=v1s[:, n, q, 0, 0:F],
                                                              op0=ALU.mult, op1=ALU.subtract)
                    last.then_inc(v1_lo, 1)

                def low_part2(n, i):
                    dve.wait_ge(v2_hi, (i - 1) * T + n + 1)
                    if n == 0:
                        nc.vector.scalar_tensor_tensor(out=v2s[:, :, 1, D], in0=E2[:], scalar=VSCALE,
                                                       in1=v2s[:, :, 0, D], op0=ALU.mult, op1=ALU.subtract)
                    nc.vector.scalar_tensor_tensor(out=v2s[:, n, 1, 0:D], in0=raw2[:, n, 0:D], scalar=E2[:, n:n + 1],
                                                   in1=v2s[:, n, 0, 0:D], op0=ALU.mult, op1=ALU.subtract).then_inc(v2_lo, 1)

                def body(i, par):
                    l1, l2, nxt = has(i)
                    for L in range(SLOTS + 2):
                        u, s = L // T, L % T
                        for n in range(T):
                            if nxt and L == proj1_slot(i, n)[1] + 1:
                                low_part_xT(i + 1, n, i)
                        for n in range(T):
                            if nxt and L == mask_slot(i, n):
                                make_mask(i + 1, 1 - par, n)
                        if split and first(i, 1) and l1 and L == L_FOLD2:
                            fold2()
                        if l1 and u == H and L - 1 in elu_slot:
                            elu(i, elu_slot.index(L - 1))
                        if l1 and u < H - 1:
                            if s == 0 and u == 0 and not first(i, 1):
                                dve.wait_ge(agg2_done, i * T)
                            if s == 0 and u > 0:
                                dve.wait_ge(agg1_done, i * S1 + u * T)
                            weights1(i, par, u + 1, s)
                        if l2 and u == H - 1:
                            if s == 0 and l1:
                                dve.wait_ge(agg1_done, i * S1 + u * T)
                            weights2(i, par, s)
                        if nxt and u == H:
                            if s == 0 and l1:
                                dve.wait_ge(agg1_done, (i + 1) * S1)
                            weights1(i + 1, 1 - par, 0, s)
                        if nxt:
                            factors1(i, par, L - L_CHAIN1)
                        if l2:
                            factors2(i, par, L - L_CHAIN2)
                        if split and not l1 and l2 and L == L_JUDGE:
                            judge()
                        if split and not l1 and l2 and L == S1 + 1:
                            decide()
                        if l1 and u < H and L - 1 in elu_slot:
                            elu(i, elu_slot.index(L - 1))
                        if l2 and 1 <= L - S1 <= T:
                            invert2(i, L - S1 - 1)
                        for n in range(T):
                            if split and nxt and L == v1_slot(i, n):
                                low_part1(n, i + 1)
                        if l2 and 1 <= L - S1 <= T:
                            residual(i, L - S1 - 1)
                        if l2 and 2 <= L - S1 <= T + 1:
                            layer_norm(i, L - S1 - 2)
                        if l2 and 1 <= L - S1 <= T:
                            moments(i, L - S1 - 1)
                        if split and l2 and 0 <= L - L_LOW2 < T:
                            low_part2(L - L_LOW2, i)

                def fold(folds, products, product_ready):
                    for n, (w, a, dst, factor) in enumerate(folds):
                        k = w.shape[-1]
                        if n >= 1:
                            dve.wait_ge(product_ready, n)
                        nc.vector.tensor_tensor_reduce(products[:, 0:k], w, a, factor, 0.0, ALU.mult, ALU.add,
                                                       dst).then_inc(product_ready, 1)
                    dve.wait_ge(product_ready, len(folds))

                def fold2():
                    dve.wait_ge(params2_loaded, 16 * 5)
                    fold([(w2[:, c, 0:D], att2[:, g * D:(g + 1) * D], w2[:, c, D + g:D + g + 1], 1.0 / VSCALE)
                          for c in range(FC) for g in range(2)], att2[:, 2 * D:3 * D], fold2_product)
                    nc.vector.memset(rden2[:], 0.0).then_inc(w2_ready, 1)
                    dve.wait_ge(w2_ready, 1)

                def start():
                    dve.wait_ge(params1_loaded, 16 * 4)
                    def column(q):
                        return q * F + (NA if q >= H // 2 else 0)

                    folds = [(w1_whole[:, c, column(q):column(q) + F], p[:, 0, 0, (g * H + q) * F:(g * H + q + 1) * F],
                              w1_whole[:, c, HF // 2 + g * H + q:HF // 2 + g * H + q + 1], 1.0)
                             for c in range(KC) for g in range(2) for q in range(H)]
                    fold(folds, p[:, 0, 1, :], fold_product)
                    for c in range(KC):
                        nc.vector.tensor_copy(w1[:, 0, c, :], w1_whole[:, c, :]).then_inc(w1_high, 1)
                    for c in range(KC):
                        dve.wait_ge(w1_high, c + 1)
                        nc.vector.tensor_tensor(w1[:, 1, c, :], w1_whole[:, c, :], w1[:, 0, c, :], ALU.subtract).then_inc(w1_parted, 1)
                    dve.wait_ge(w1_parted, KC)
                    nc.vector.memset(rden[:], 0.0).then_inc(w1_ready, 1)
                    dve.wait_ge(w1_ready, 1)
                    nc.vector.memset(bounds[:, 0, :], 0.0).then_inc(bounds1_taken, 1)
                    nc.vector.memset(bounds[:, 1, :], SPLIT_LARGE).then_inc(bounds2_taken, 1)
                    nc.vector.memset(bounds[:, 2, :], 0.0).then_inc(bounds2_taken, 1)
                    dve.wait_ge(bounds2_taken, 2)

                def judge():
                    dve.wait_ge(bounds1_taken, 5 * B + 1)
                    dve.wait_ge(bounds2_taken, 5 * B + 2)
                    least = bounds[:, 1:3, :].rearrange("p k l -> p (k l)")
                    nc.vector.tensor_scalar(least, least, -1.0, None, ALU.mult).then_inc(bounds_ready, 1)

                def decide():
                    dve.wait_ge(bounds_reduced, 1)
                    for k, limit in enumerate((SPLIT_LARGE, -SPLIT_SMALL, SPLIT_SPREAD)):
                        nc.vector.tensor_scalar(within[:, 2 * k:2 * k + 2], bounds_all[:, k, :], limit, None,
                                                ALU.is_le).then_inc(compared, 1)
                    dve.wait_ge(compared, 3)
                    nc.vector.tensor_reduce(verdict[:], within[:], AX.X, ALU.min)

                def program():
                    if split:
                        start()
                    run(dve, body)

                when_needed(dve, program)

        for split in (True, False):
            semaphores = []
            with ExitStack() as pass_ctx:
                one_pass(split, pass_ctx, semaphores)
            nc.clear_and_free_semaphores(semaphores)
            nc.all_engine_barrier()


_INS = ["x", "adj", "L0_gnn_W1", "L0_gnn_att_src1", "L0_gnn_att_dst1", "L0_gnn_b1", "L0_gnn_W2", "L0_gnn_att_src2",
        "L0_gnn_att_dst2", "L0_gnn_b2"]
_OUTS = [((8, 1024, 256), "float32")]


def kernel(**inputs):
    import numpy as _np
    import concourse.bacc as _bacc
    from concourse import mybir as _mybir
    from concourse.bass_utils import run_bass_kernel_spmd as _run

    nc = _bacc.Bacc("TRN2", target_bir_lowering=False, num_devices=1)
    arrays, args = {}, []
    for name in _INS:
        a = _np.ascontiguousarray(inputs[name])
        arrays[f"in_{name}_dram"] = a
        args.append(nc.dram_tensor(f"in_{name}_dram", a.shape, _mybir.dt.from_np(a.dtype), kind="ExternalInput").ap())
    for i, (shape, dtype) in enumerate(_OUTS):
        dt = _mybir.dt.from_np(_np.dtype(dtype))
        args.append(nc.dram_tensor(f"out_{i}_dram", shape, dt, kind="ExternalOutput").ap())
    build_gat(nc, *args)
    r = _run(nc, [arrays], core_ids=[0])
    got = tuple(r.results[0][f"out_{i}_dram"] for i in range(len(_OUTS)))
    return got[0]
```
